# Optimizing a Trainium2 kernel written in Bass

```python
import numpy as np
import jax
import jax.numpy as jnp

def _softmax(x, axis=-1):
    return jax.nn.softmax(x, axis=axis)

def _gelu(x):
    return jax.nn.gelu(x, approximate=True)

def _silu(x):
    return jax.nn.silu(x)

def _sigmoid(x):
    return jax.nn.sigmoid(x)

def _layernorm(x, axis=-1, eps=1e-05):
    m = jnp.mean(x, axis=axis, keepdims=True)
    v = jnp.var(x, axis=axis, keepdims=True)
    return (x - m) / jnp.sqrt(v + eps)

def _scatter_add(tgt, idx, src, axis=0):
    return tgt.at[idx].add(src)

def _segment_sum(src, seg, n):
    return jax.ops.segment_sum(src, seg, n)
kernel_name = 'mk_gnn_resnorm_d4_gnn_r32_19a5b2'

def setup_inputs(seed: int=0):
    np.random.seed(seed)
    _w = jnp.asarray

    def _rec_inputs():
        import jax
        import jax.numpy as jnp
        _gk = jax.random.key(seed)
        x = -0.0001006 + 1 * jax.random.normal(jax.random.fold_in(_gk, 1), (50000, 96), jnp.float32)
        src = jax.random.randint(jax.random.fold_in(_gk, 2), (25000,), 0, 50000, jnp.int32)
        dst = jnp.minimum((50000 * jax.random.uniform(jax.random.fold_in(_gk, 3), (25000,)) ** 2.0).astype(jnp.int32), 49999)
        _o = jnp.argsort(dst, stable=True)
        src = src[_o]
        dst = dst[_o]
        edge_attr_32 = 0.000196303 + 1.00016 * jax.random.normal(jax.random.fold_in(_gk, 12), (25000, 32), jnp.float32)
        return (x, src, dst, edge_attr_32)
    x, src, dst, edge_attr_32 = _rec_inputs()

    def _L0_gnn_setup():
        import jax, jax.numpy as jnp
        import numpy as np
        N_NODES = 50000
        EPS = 0.0
        key = jax.random.key(seed)
        k1, k2, k3, k4, k5 = jax.random.split(key, 5)
        d = 96
        E = 25000
        feat = jax.random.normal(k1, (N_NODES, d), dtype=jnp.float32)
        W1 = jax.random.normal(k2, (d, d), dtype=jnp.float32) * (1.0 / np.sqrt(d))
        b1 = jnp.zeros((d,), dtype=jnp.float32)
        W2 = jax.random.normal(k3, (d, d), dtype=jnp.float32) * (1.0 / np.sqrt(d))
        b2 = jnp.zeros((d,), dtype=jnp.float32)
        edge_src = jax.random.randint(k4, (E,), 0, N_NODES, dtype=jnp.int64)
        edge_dst = jax.random.randint(k5, (E,), 0, N_NODES, dtype=jnp.int64)
        return {'feat': feat, 'W1': W1, 'b1': b1, 'W2': W2, 'b2': b2, 'edge_src': edge_src, 'edge_dst': edge_dst}
    _L0_gnn_all = _L0_gnn_setup()
    _L0_gnn_in = {k: v for k, v in _L0_gnn_all.items() if k in ('W1', 'b1', 'W2', 'b2')}
    del _L0_gnn_all

    def _L1_gnn_setup():
        import jax, jax.numpy as jnp
        import numpy as np
        K = 16
        ALPHA = 0.1
        key = jax.random.key(seed)
        k1, k2 = jax.random.split(key)
        N, E, D = (50000, 25000, 96)
        x = jax.random.normal(k1, (N, D), dtype=jnp.float32)
        edge_index = jax.random.randint(k2, (2, E), 0, N, dtype=jnp.int64)
        return {'x': x, 'edge_index': edge_index}
    _L1_gnn_all = _L1_gnn_setup()
    _L1_gnn_in = {k: v for k, v in _L1_gnn_all.items() if k in ()}
    del _L1_gnn_all

    def _L2_gnn_setup():
        import jax, jax.numpy as jnp
        import numpy as np
        N, E = (50000, 25000)
        DIN = DOUT = 96
        DE = 32

        def _egnn_conv(x, src, dst, edge_attr, W_msg, W_edge, W_root, b):
            msg = x[src] @ W_msg + edge_attr @ W_edge
            agg = jax.ops.segment_max(msg, dst, num_segments=x.shape[0])
            agg = jnp.where(jnp.isneginf(agg), 0.0, agg)
            return agg + x @ W_root + b
        key = jax.random.key(seed)
        ks = jax.random.split(key, 10)
        rn = lambda k, sh, sc: jax.random.normal(k, sh, jnp.float32) * sc
        return {'X': rn(ks[0], (N, DIN), 1.0), 'edge_index': jax.random.randint(ks[1], (2, E), 0, N, jnp.int32), 'edge_attr': rn(ks[2], (E, DE), 1.0), 'W1_msg': rn(ks[3], (DIN, DOUT), DIN ** (-0.5)), 'W1_edge': rn(ks[4], (DE, DOUT), DE ** (-0.5)), 'W1_root': rn(ks[5], (DIN, DOUT), DIN ** (-0.5)), 'b1': jnp.zeros((DOUT,), jnp.float32), 'W2_msg': rn(ks[6], (DOUT, DOUT), DOUT ** (-0.5)), 'W2_edge': rn(ks[7], (DE, DOUT), DE ** (-0.5)), 'W2_root': rn(ks[8], (DOUT, DOUT), DOUT ** (-0.5)), 'b2': jnp.zeros((DOUT,), jnp.float32)}
    _L2_gnn_all = _L2_gnn_setup()
    _L2_gnn_in = {k: v for k, v in _L2_gnn_all.items() if k in ('W1_msg', 'W1_edge', 'W1_root', 'b1', 'W2_msg', 'W2_edge', 'W2_root', 'b2')}
    del _L2_gnn_all

    def _L3_gnn_setup():
        import jax, jax.numpy as jnp
        import numpy as np
        N, C, E = (50000, 96, 25000)
        SCALES = (2, 3, 4)
        BN_EPS = 1e-05

        def _cheb(x, prop, w, b):
            K = w.shape[0]
            Tx0 = x
            out = Tx0 @ w[0]
            if K > 1:
                Tx1 = prop(Tx0)
                out = out + Tx1 @ w[1]
                for k in range(2, K):
                    Tx2 = 2.0 * prop(Tx1) - Tx0
                    out = out + Tx2 @ w[k]
                    Tx0, Tx1 = (Tx1, Tx2)
            return out + b
        key = jax.random.key(seed)
        ks = jax.random.split(key, 16)
        inp = {'x': jax.random.normal(ks[0], (N, C), dtype=jnp.float32), 'edge_index': jax.random.randint(ks[1], (2, E), 0, N, dtype=jnp.int64)}
        s = 1.0 / np.sqrt(C)
        for i, k in enumerate(SCALES):
            inp[f'w{k}'] = jax.random.uniform(ks[2 + 2 * i], (k, C, C), jnp.float32, -s, s)
            inp[f'b{k}'] = jax.random.uniform(ks[3 + 2 * i], (C,), jnp.float32, -s, s)
        s3 = 1.0 / np.sqrt(3 * C)
        inp['attn_w'] = jax.random.uniform(ks[8], (3 * C, 3), jnp.float32, -s3, s3)
        inp['attn_b'] = jax.random.uniform(ks[9], (3,), jnp.float32, -s3, s3)
        inp['fus_w'] = jax.random.uniform(ks[10], (3 * C, C), jnp.float32, -s3, s3)
        inp['fus_b'] = jax.random.uniform(ks[11], (C,), jnp.float32, -s3, s3)
        inp['bn_gamma'] = jnp.ones((C,), jnp.float32)
        inp['bn_beta'] = jnp.zeros((C,), jnp.float32)
        return inp
    _L3_gnn_all = _L3_gnn_setup()
    _L3_gnn_in = {k: v for k, v in _L3_gnn_all.items() if k in ('w2', 'b2', 'w3', 'b3', 'w4', 'b4', 'attn_w', 'attn_b', 'fus_w', 'fus_b', 'bn_gamma', 'bn_beta')}
    del _L3_gnn_all
    return {'x': x, 'src': src, 'dst': dst, 'edge_attr_32': edge_attr_32, 'L0_gnn_W1': _L0_gnn_in['W1'], 'L0_gnn_b1': _L0_gnn_in['b1'], 'L0_gnn_W2': _L0_gnn_in['W2'], 'L0_gnn_b2': _L0_gnn_in['b2'], 'L2_gnn_W1_msg': _L2_gnn_in['W1_msg'], 'L2_gnn_W1_edge': _L2_gnn_in['W1_edge'], 'L2_gnn_W1_root': _L2_gnn_in['W1_root'], 'L2_gnn_b1': _L2_gnn_in['b1'], 'L2_gnn_W2_msg': _L2_gnn_in['W2_msg'], 'L2_gnn_W2_edge': _L2_gnn_in['W2_edge'], 'L2_gnn_W2_root': _L2_gnn_in['W2_root'], 'L2_gnn_b2': _L2_gnn_in['b2'], 'L3_gnn_w2': _L3_gnn_in['w2'], 'L3_gnn_b2': _L3_gnn_in['b2'], 'L3_gnn_w3': _L3_gnn_in['w3'], 'L3_gnn_b3': _L3_gnn_in['b3'], 'L3_gnn_w4': _L3_gnn_in['w4'], 'L3_gnn_b4': _L3_gnn_in['b4'], 'L3_gnn_attn_w': _L3_gnn_in['attn_w'], 'L3_gnn_attn_b': _L3_gnn_in['attn_b'], 'L3_gnn_fus_w': _L3_gnn_in['fus_w'], 'L3_gnn_fus_b': _L3_gnn_in['fus_b'], 'L3_gnn_bn_gamma': _L3_gnn_in['bn_gamma'], 'L3_gnn_bn_beta': _L3_gnn_in['bn_beta']}

def reference(x, src, dst, edge_attr_32, L0_gnn_W1, L0_gnn_b1, L0_gnn_W2, L0_gnn_b2, L2_gnn_W1_msg, L2_gnn_W1_edge, L2_gnn_W1_root, L2_gnn_b1, L2_gnn_W2_msg, L2_gnn_W2_edge, L2_gnn_W2_root, L2_gnn_b2, L3_gnn_w2, L3_gnn_b2, L3_gnn_w3, L3_gnn_b3, L3_gnn_w4, L3_gnn_b4, L3_gnn_attn_w, L3_gnn_attn_b, L3_gnn_fus_w, L3_gnn_fus_b, L3_gnn_bn_gamma, L3_gnn_bn_beta):
    import jax
    import jax.numpy as jnp

    def _L0_gnn_ref(feat, W1, b1, W2, b2, edge_src, edge_dst):
        import jax, jax.numpy as jnp
        import numpy as np
        N_NODES = 50000
        EPS = 0.0
        msg = feat[edge_src]
        neigh = jax.ops.segment_sum(msg, edge_dst, num_segments=N_NODES)
        rst = (1.0 + EPS) * feat + neigh
        h = jax.nn.relu(rst @ W1 + b1)
        out = h @ W2 + b2
        return out

    def _L1_gnn_ref(x, edge_index):
        import jax, jax.numpy as jnp
        import numpy as np
        K = 16
        ALPHA = 0.1
        N = x.shape[0]
        loop = jnp.arange(N, dtype=edge_index.dtype)
        row = jnp.concatenate([edge_index[0], loop])
        col = jnp.concatenate([edge_index[1], loop])
        deg = jax.ops.segment_sum(jnp.ones_like(col, dtype=x.dtype), col, num_segments=N)
        deg_inv_sqrt = jnp.where(deg > 0, jax.lax.rsqrt(jnp.maximum(deg, 1e-30)), 0.0)
        norm = (deg_inv_sqrt[row] * deg_inv_sqrt[col])[:, None]
        h = x
        for _ in range(K):
            h_neighbors = jax.ops.segment_sum(norm * h[row], col, num_segments=N)
            h = (1.0 - ALPHA) * h_neighbors + ALPHA * x
        return h

    def _L2_gnn_ref(X, edge_index, edge_attr, W1_msg, W1_edge, W1_root, b1, W2_msg, W2_edge, W2_root, b2):
        import jax, jax.numpy as jnp
        import numpy as np
        N, E = (50000, 25000)
        DIN = DOUT = 96
        DE = 32

        def _egnn_conv(x, src, dst, edge_attr, W_msg, W_edge, W_root, b):
            msg = x[src] @ W_msg + edge_attr @ W_edge
            agg = jax.ops.segment_max(msg, dst, num_segments=x.shape[0])
            agg = jnp.where(jnp.isneginf(agg), 0.0, agg)
            return agg + x @ W_root + b
        src, dst = (edge_index[0], edge_index[1])
        c1 = jax.nn.leaky_relu(_egnn_conv(X, src, dst, edge_attr, W1_msg, W1_edge, W1_root, b1))
        c2 = jax.nn.leaky_relu(_egnn_conv(c1, src, dst, edge_attr, W2_msg, W2_edge, W2_root, b2))
        return c2

    def _L3_gnn_ref(x, edge_index, w2, b2, w3, b3, w4, b4, attn_w, attn_b, fus_w, fus_b, bn_gamma, bn_beta):
        import jax, jax.numpy as jnp
        import numpy as np
        N, C, E = (50000, 96, 25000)
        SCALES = (2, 3, 4)
        BN_EPS = 1e-05

        def _cheb(x, prop, w, b):
            K = w.shape[0]
            Tx0 = x
            out = Tx0 @ w[0]
            if K > 1:
                Tx1 = prop(Tx0)
                out = out + Tx1 @ w[1]
                for k in range(2, K):
                    Tx2 = 2.0 * prop(Tx1) - Tx0
                    out = out + Tx2 @ w[k]
                    Tx0, Tx1 = (Tx1, Tx2)
            return out + b
        n = x.shape[0]
        row, col = (edge_index[0], edge_index[1])
        deg = jax.ops.segment_sum(jnp.ones(row.shape[0], x.dtype), row, num_segments=n)
        dis = jnp.where(deg > 0, jax.lax.rsqrt(jnp.maximum(deg, 1.0)), 0.0)
        wn = -(dis[row] * dis[col])

        def prop(h):
            return jax.ops.segment_sum(wn[:, None] * h[row], col, num_segments=n)
        feats = [_cheb(x, prop, w2, b2), _cheb(x, prop, w3, b3), _cheb(x, prop, w4, b4)]
        concat = jnp.concatenate(feats, axis=1)
        scale_w = jax.nn.softmax(concat @ attn_w + attn_b, axis=1)
        fused = jnp.concatenate([feats[i] * scale_w[:, i:i + 1] for i in range(3)], axis=1)
        h = fused @ fus_w + fus_b
        mean = jnp.mean(h, axis=0)
        var = jnp.mean((h - mean) ** 2, axis=0)
        h = (h - mean) * jax.lax.rsqrt(var + BN_EPS) * bn_gamma + bn_beta
        return jax.nn.relu(h)
    edge_index = jnp.stack([src, dst])
    x = _layernorm(x + _L0_gnn_ref(x, L0_gnn_W1, L0_gnn_b1, L0_gnn_W2, L0_gnn_b2, src, dst), axis=-1)
    x = _layernorm(x + _L1_gnn_ref(x, edge_index), axis=-1)
    x = _layernorm(x + _L2_gnn_ref(x, edge_index, edge_attr_32, L2_gnn_W1_msg, L2_gnn_W1_edge, L2_gnn_W1_root, L2_gnn_b1, L2_gnn_W2_msg, L2_gnn_W2_edge, L2_gnn_W2_root, L2_gnn_b2), axis=-1)
    x = _layernorm(x + _L3_gnn_ref(x, edge_index, L3_gnn_w2, L3_gnn_b2, L3_gnn_w3, L3_gnn_b3, L3_gnn_w4, L3_gnn_b4, L3_gnn_attn_w, L3_gnn_attn_b, L3_gnn_fus_w, L3_gnn_fus_b, L3_gnn_bn_gamma, L3_gnn_bn_beta), axis=-1)
    return x

_drawn_inputs = setup_inputs


def setup_inputs(seed=0):
    import zlib

    import numpy as np

    out = dict(_drawn_inputs(seed))
    spreads = {'L0_gnn_b1': (0.0, 0.1),
     'L0_gnn_b2': (0.0, 0.1),
     'L2_gnn_b1': (0.0, 0.1),
     'L2_gnn_b2': (0.0, 0.1),
     'L3_gnn_bn_gamma': (1.0, 0.2),
     'L3_gnn_bn_beta': (0.0, 0.1)}
    factors = {'L3_gnn_b2': 6.701,
     'L3_gnn_b3': 7.174,
     'L3_gnn_b4': 4.165,
     'L3_gnn_attn_b': 6.362,
     'L3_gnn_fus_b': 8.0}
    for name, (base, spread) in spreads.items():
        noise = np.random.default_rng([zlib.crc32(name.encode()), seed]).standard_normal(out[name].shape)
        drawn = base * np.exp(spread * noise) if base else spread * noise
        out[name] = jnp.asarray(drawn.astype(out[name].dtype))
    for name, factor in factors.items():
        out[name] = (out[name] * factor).astype(out[name].dtype)
    return out
```

```python
import concourse.bass as bass
from concourse import mybir
from contextlib import ExitStack

F32 = mybir.dt.float32
F16 = mybir.dt.float16
BF16 = mybir.dt.bfloat16
I32 = mybir.dt.int32
U8 = mybir.dt.uint8
ALU = mybir.AluOpType
ACT = mybir.ActivationFunctionType
AX = mybir.AxisListType

N, E, C, DE = 50000, 25000, 96, 32
P = 128
Q = 4
GRP = P * Q
GROUPS = -(-E // GRP)
TILES = -(-N // GRP)
EP, NP = GROUPS * GRP, TILES * GRP
R = 7
GI, TI = GROUPS // R, TILES // R
assert GI * R == GROUPS and TI * R == TILES
QC = Q * C
FW = 3 * C + 3
TW = 100
HOPS = 16
ALPHA = 0.1
KEEP = 1.0 - ALPHA
EPS = 1e-5
BIG = 3.0e38
FAR = 1 << 17
IDX = GROUPS * Q


def build(nc, t):
    ctx = ExitStack()
    with ctx:
        sb = lambda n, s, d=F32: ctx.enter_context(nc.sbuf_tensor(n, s, d))
        pb = lambda n: ctx.enter_context(nc.psum_tensor(n, [P, 512], F32))
        sem = lambda n: ctx.enter_context(nc.semaphore(n))
        dram = lambda n, s: nc.dram_tensor(n, s, F32, kind="Internal").ap()

        aug = dram("aug", (NP, TW))
        hop_tab = dram("hop_tab", (NP + 2 * EP, C))
        x2_tab = dram("x2_tab", (NP, C))
        c1_tab = dram("c1_tab", (NP, C))
        x3_tab = dram("x3_tab", (NP, C))
        u3_tab = dram("u3_tab", (NP, C))
        agg_tab = dram("agg_tab", (NP, C))
        q_tab = [dram("q1_tab", (EP + GRP, C)), dram("q2_tab", (EP + GRP, C))]
        p_slot = dram("p_slot", (EP, 2 * C))
        f_tab = dram("f_tab", (NP, FW))
        h_tab = dram("h_tab", (NP, C))
        sc_keep_dram = dram("out_sc_keep", (P, TILES * Q))

        ident = sb("ident", [P, P])
        keep = sb("keep", [P, EP], U8)
        src_i = sb("src_i", [P, IDX], I32)
        dst_i = sb("dst_i", [P, IDX], I32)
        put_i = sb("put_i", [P, IDX], I32)
        hop_i = [sb("hopa_i", [P, IDX], I32), sb("hopb_i", [P, IDX], I32)]
        q_i = sb("q_i", [P, IDX], I32)
        sd_in = sb("sd_in", [P, IDX])
        w_hop = sb("w_hop", [P, IDX])
        w_out = sb("w_out", [P, IDX])
        node_sc = sb("node_sc", [P, 3, TILES * Q])
        get_st = sb("get_st", [P, R, Q], I32)
        put_st = sb("put_st", [P, R, Q], I32)
        G = sb("G", [P, R, Q * TW])
        sc = sb("sc", [P, 3, GRP])
        eps_col = sb("eps_col", [P, 1])
        tmp = sb("tmp", [P, 2, QC])
        out_r = sb("out_r", [P, R, QC])
        out_rows = [out_r[:, j, :] for j in range(R)]
        big = sb("big", [P, 2, IDX * C])
        state, g0 = big[:, 0, :], big[:, 1, :]

        def carve(at, cols, parts=P):
            flat = big[:, :, :].rearrange("p a n -> p (a n)")
            assert at + cols <= 2 * IDX * C
            return flat[0:parts, at:at + cols]

        ps = ctx.enter_context(nc.psum_tensor("ps", [P, 8, 512], F32))
        bank = [ps[:, b, :] for b in range(8)]
        pin, pout, pmm = bank[0:3], bank[3:6], bank[6:8]

        setup_ld = sem("setup_ld")
        bar = sem("bar")
        chain_s = {e: sem("chain_" + e) for e in ("dve", "act", "pool")}
        got = [sem(f"got{j}") for j in range(R)]
        put = [sem(f"put{j}") for j in range(R)]
        staged = sem("staged")
        put_staged = sem("put_staged")
        taken = sem("taken")
        moved = sem("moved")
        mixed = sem("mixed")
        scanned = sem("scanned")
        tout = sem("tout")
        done = sem("done")
        freed = sem("freed")
        keeps = sem("keeps")
        pool_turn = sem("pool_turn")
        wr = [sem(f"wr{j}") for j in range(R)]
        ld = [sem(f"ld{j}") for j in range(R)]
        st = [sem(f"st{j}") for j in range(R)]

        def ge(eng, s, v):
            if isinstance(v, int) and v <= 0:
                return
            eng.wait_ge(s, v)

        class Chain:
            def __init__(self, eng, name, at=0):
                self.eng, self.s, self.at, self.n = eng, chain_s[name], at, 0

            def step(self, ins):
                ins.then_inc(self.s, 1)
                self.n += 1
                self.eng.wait_ge(self.s, self.at + self.n)

        chain_at = {"dve": 0, "act": 0, "pool": 0}

        def straight(eng, name):
            return Chain(eng, name, chain_at[name])

        def end_straight(ch, name):
            chain_at[name] += ch.n

        def loop(eng, n, body, name=None, steps=0, first=True):
            at = chain_at[name] if name else 0

            def once(i):
                ch = Chain(eng, name, at + steps * i) if name else None
                body(i, ch)
                assert ch is None or ch.n == steps, (ch.n, steps)
            lo = 0
            if first:
                once(0)
                lo = 1
            if n > lo:
                with eng.Fori(lo, n) as i:
                    once(i)
            if name:
                chain_at[name] += steps * n

        barriers = {"n": {}}

        def barrier(eng, name):
            k = barriers["n"].get(name, 0) + 1
            barriers["n"][name] = k
            eng.drain().then_inc(bar, 1)
            eng.wait_ge(bar, 5 * k)


        S3, GAP3 = [0, 1, 0, 1, 0, 1, 2], [3, 3, 2, 2, 2, 2, 7]
        S2, GAP2 = [0, 1, 0, 1, 0, 1, 0], [1, 3, 2, 2, 2, 2, 2]

        def rows(tab, i, j, base=0, w=None):
            part = tab[bass.ds(i * (R * GRP) + (j * GRP + base), GRP), :]
            if w is not None:
                part = part[:, w[0]:w[1]]
            return part.rearrange("(p q) c -> p q c", p=P)

        def at(i, j, w, n=None, off=0):
            return bass.ds(i * (R * w) + (j * w + off), n or w)

        def v3(ap, w=C):
            return ap.rearrange("p (q c) -> p q c", c=w)

        def spread(ap):
            return ap.unsqueeze(2).to_broadcast([P, Q, C])

        SUM0, DSTS, HOP1, HOP2, HOPL, MAX1, MAX2, CHEB1, CHEB2, CHEB3 = 0, 1, 2, 3, 17, 18, 19, 20, 21, 22
        ROUNDS = (HOPL - HOP2) // 2

        def scans(k):
            return k if isinstance(k, int) and k <= DSTS else k - 1

        SCATTERS = (SUM0, HOPL, MAX1, MAX2, CHEB3)
        TABLES = {k: 0 for k in (SUM0, DSTS, HOPL, MAX1, MAX2, CHEB3)}

        def lagged(i, j, lag):
            if j >= lag:
                return i, j - lag
            return (None, None) if isinstance(i, int) and i == 0 else (i - 1, j - lag + R)

        def pipeline(eng, n, stages, name=None, steps=0, peel=True):
            top = max(lag for lag, _ in stages)
            base = chain_at[name] if name else 0
            per = steps

            def body(i, upto=R, tail=False):
                full = not (isinstance(i, int) and i == 0) and not tail
                ch = None
                if name:
                    start = base if isinstance(i, int) and i == 0 else base + (firstn["n"] + (i - 1) * per if not tail else firstn["n"] + (n - 1) * per)
                    ch = Chain(eng, name, start)
                for j in range(upto):
                    for lag, f in stages:
                        if tail and j >= lag:
                            continue
                        a, b = lagged(i, j, lag)
                        if a is not None:
                            f(a, b, ch)
                return ch
            firstn = {"n": 0}
            ch = body(0)
            if ch:
                firstn["n"] = ch.n
            if n > 1:
                with eng.Fori(1, n) as i:
                    ch = body(i)
                    assert ch is None or ch.n == per, (name, ch.n, per)
            tail = body(n, upto=top, tail=True)
            if name:
                chain_at[name] = base + firstn["n"] + (n - 1) * per + tail.n

        def bases(table):
            out, total = {}, 0
            for phase, per, n in table:
                out[phase] = total
                total += 16 * per * n
            return out, total

        LD, LD_ALL = bases([("keep", 1, GI), ("gin", 2, TI), ("appnp", 2, TI), ("max1", 1, GI), ("conv1", 2, TI),
                            ("max2", 1, GI), ("conv2", 3, TI), ("cheb3", 1, GI), ("attend", 2, TI), ("norm", 2, TI)])
        ST, ST_ALL = bases([("gin", 2, TI), ("appnp", 1, TI), ("conv1", 1, TI), ("conv2", 2, TI), ("attend", 1, TI),
                            ("norm", 1, TI)])
        WR, WR_ALL = bases([("hops", 1, GI * HOPS), ("cheb1", 2, GI), ("cheb2", 2, GI)])
        PUT, PUT_ALL = bases([(k, Q, GI) for k in SCATTERS])

        def ring(start, cols, n=R, parts=P):
            return [carve(start + s * cols, cols, parts) for s in range(n)], start + n * cols

        lay = {}
        edge_f, o = ring(0, 4 * IDX, 1)
        lo_hi = edge_f[0].rearrange("p (k n) -> p k n", k=4)
        onehot, o = ring(o, 2 * (GRP + P) // 2, Q)
        keep_ld, o = ring(o, GRP + 1)
        iota_lo, o = ring(o, GRP // 2, 1)
        iota_hi, o = ring(o, P // 2, 1)
        zeros, o = ring(o, Q * 3 * C, 1)
        node_sc_, o = ring(o, 3 * TILES * Q, 1)
        node_sc = node_sc_[0].rearrange("p (k n) -> p k n", k=3)
        deg, o = ring(o, GRP, 10)
        tri, o = ring(o, P, 1)
        gin0 = o
        w_gin1, o = ring(o, C, 1)
        w_gin2, o = ring(o, C, 1)
        b_gin1, o = ring(o, 1, 1)
        gin_x, o = ring(o, QC)
        gin_z, o = ring(o, QC)
        gin_r, o = ring(o, GRP, 3)
        gin_h, o = ring(o, GRP, 3)
        gin_y, o = ring(o, QC)
        gin_s, o = ring(o, 4 * Q)
        gin_sq, o = ring(o, QC, 3)
        gin_o, o = ring(o, QC)
        gin_a, o = ring(o, Q * TW)
        o = 0
        out_sc_, o = ring(o, TILES * Q, 1)
        neg, o = ring(o, EP // 2, 1)
        neg = neg[0].bitcast(BF16)
        w_mix, o = ring(o, C, 2)
        w_root, o = ring(o, C, 2)
        mix_r, o = ring(o, GRP, 3)
        late0 = o
        d_x, o = ring(o, QC)
        d_z, o = ring(o, QC)
        d_w, o = ring(o, QC)
        d_t, o = ring(o, GRP, 3)
        d_y, o = ring(o, QC)
        d_s, o = ring(o, 4 * Q)
        d_sq, o = ring(o, QC, 3)
        d_o, o = ring(o, QC)
        d_u, o = ring(o, QC)
        zeros2, _ = ring(late0, 2 * Q * FW, 1)
        o = late0
        w_feat, o = ring(o, FW, 4)
        bn, o = ring(o, 16, 1)
        late1 = o
        cheb_a, o = ring(o, QC)
        cheb_b, o = ring(o, QC)
        cheb_p, o = ring(o, 3 * QC, 3)
        cheb_t, o = ring(o, GRP, 6)
        cheb_f, o = ring(o, Q * FW)
        o = late1
        a_x, o = ring(o, QC)
        a_f, o = ring(o, Q * FW)
        a_t, o = ring(o, GRP, 3)
        a_h, o = ring(o, QC)
        a_s, o = ring(o, 8 * Q)
        stats, o = ring(o, TILES * 6, 1)
        assert o < late1 + 20000
        bn_wide, o = ring(late1 + 20000, P, 2)
        bn_row, o = ring(o, 2 * C, 1)
        o = late1
        wt, o = ring(o, 9 * C, 1)
        wh, o = ring(o, 9 * (C + 1), 1)
        wb, o = ring(o, 3, 1)
        att, o = ring(o, 9, 1)
        fus, o = ring(o, 3 * C, 1)
        att_b, o = ring(o, FW, 1)
        FEATS = [((0, 1), 195), ((0, 1, 2), 99), ((0, 1, 2, 3), 0)]
        LOGIT, WIDE, filt_at = C, [291, 291, 195, 99], [0, 2, 5]

        dsem = {(ph, n): sem(f"{ph}_{n}") for ph, ns in {
            "gin": "summed turned copied mixed1 relued mixed2 used centred squared reduced rooted final",
            "appnp": "used centred squared reduced rooted final",
            "conv1": "turned copied mixed2 used final",
            "conv2": "turned copied mixed2 used centred squared reduced rooted final",
            "attend": "turned copied mixed2 topped raised summed scaled shared used turned2 final",
            "norm": "used centred squared reduced rooted final"}.items() for n in ns.split()}
        one = {n: sem(n) for n in "idents hot histed cleared puts zeroed step_pe step_dve step_act prep_ld ones_set".split()}
        table_written = sem("table_written")
        fturned = sem("fturned")
        fcopied = sem("fcopied")
        fmixed = sem("fmixed")
        thirds = sem("thirds")
        fread = sem("fread")
        outdone = sem("outdone")
        put_ready = sem("put_ready")
        KU = {SUM0: 0, HOPL: 1, MAX1: 2, MAX2: 3, CHEB3: 4}
        OUTD = (HOPL, CHEB3)

        FBANK, FGAP = [4, 5, 4], [1, 3, 2]
        FCREDIT = 4 * 2
        nload = {"gin": 2, "conv1": 2, "conv2": 3}

        def cnt(i, j):
            return i * R + j

        block = ctx.enter_context(nc.Block())

        @block.sync
        def _(sp):
            sp.dma_start(src_i[:, :], t["src"].rearrange("(t p q) -> p t q", p=P, q=Q)).then_inc(setup_ld, 16)
            sp.dma_start(dst_i[:, :], t["dst"][1:EP + 1].rearrange("(t p q) -> p t q", p=P, q=Q)).then_inc(setup_ld, 16)
            sp.dma_start(put_i[:, :], t["dst"][2:EP + 2].rearrange("(t p q) -> p t q", p=P, q=Q)).then_inc(setup_ld, 16)
            sp.dma_start(w_gin1[0][0:C, :], t["gin_w1"]).then_inc(setup_ld, 16)
            sp.dma_start(w_gin2[0][0:C, :], t["gin_w2"]).then_inc(setup_ld, 16)
            sp.dma_start(w_gin2[0][C:C + 1, :], t["gin_b2"].rearrange("(o c) -> o c", o=1)).then_inc(setup_ld, 16)
            sp.dma_start(b_gin1[0][0:C, :], t["gin_b1"].rearrange("(c o) -> c o", o=1)).then_inc(setup_ld, 16)

            def load_dst(i, j, ch):
                ge(sp, keeps, cnt(i, j) - R + 1)
                sp.dma_start(keep_ld[j].bitcast(I32)[0:C, :], t["dst"][bass.ds(i * (R * GRP) + j * GRP, GRP + 1)].partition_broadcast(C)).then_inc(ld[j], 16)
            pipeline(sp, GI, [(0, load_dst)])
            barrier(sp, "sp")
            barrier(sp, "sp")
            sp.dma_start(sc_keep_dram, node_sc[:, 2, :]).then_inc(one["prep_ld"], 16)

            for q in q_tab:
                sp.dma_start(q[EP:EP + GRP, :].rearrange("(p q) c -> p q c", p=P), v3(zeros[0][:, 0:QC])).then_inc(one["zeroed"], 16)
            sp.wait_ge(one["prep_ld"], 16)
            sp.wait_ge(one["zeroed"], 16 * (TILES + 2))

            def dense(ph, loads, stores, per=1):
                def load(i, j, ch):
                    ge(sp, dsem[ph, "used"], per * (cnt(i, j) - R + 1))
                    for dst, src, w in loads:
                        sp.dma_start(v3(dst[j], w), rows(src, i, j)).then_inc(ld[j], 16)

                def store(i, j, ch):
                    ge(sp, dsem[ph, "final"], cnt(i, j) + 1)
                    for src, dst, w in stores:
                        sp.dma_start(rows(dst, i, j), v3(src[j], w)).then_inc(st[j], 16)
                pipeline(sp, TI, [(0, load), (R, store)])
                for j in range(R):
                    sp.wait_ge(st[j], ST[ph] + 16 * len(stores) * TI)
                barrier(sp, "sp")

            dense("gin", [(gin_x, t["x"], C), (gin_z, agg_tab, C)], [(gin_o, hop_tab, C), (gin_a, aug, TW)])
            barrier(sp, "sp")

            def hop_store(k, h, parity):
                def store(i, j):
                    sp.wait_ge(done, h * GROUPS + cnt(i, j) + 1)
                    for n in ((0, 1) if k == HOP1 else (parity,)):
                        sp.dma_start(rows(hop_tab, i, j, NP + n * EP), v3(state[:, at(i, j, QC)])).then_inc(wr[j], 16)
                with sp.Fori(0, GI) as i:
                    for j in range(R):
                        store(i, j)
                for j in range(R):
                    sp.wait_ge(wr[j], h * (16 * GI) + 32 * GI)
                sp.sem_inc(table_written, 1)
            hop_store(HOP1, 0, 0)
            barrier(sp, "sp")
            with sp.Fori(0, ROUNDS) as r:
                hop_store(None, r * 2 + 1, 1)
                hop_store(None, r * 2 + 2, 0)
            barrier(sp, "sp")

            sp.dma_start(out_sc_[0], sc_keep_dram).then_inc(one["prep_ld"], 16)
            for n in range(2):
                sp.dma_start(w_mix[n][0:C, :], t[f"conv{n}_msg"]).then_inc(one["prep_ld"], 16)
                sp.dma_start(w_mix[n][C:P, :], t[f"conv{n}_edge"]).then_inc(one["prep_ld"], 16)
                sp.dma_start(w_root[n][0:C, :], t[f"conv{n}_root"]).then_inc(one["prep_ld"], 16)
                sp.dma_start(w_root[n][C:C + 1, :], t[f"conv{n}_b"].rearrange("(o c) -> o c", o=1)).then_inc(one["prep_ld"], 16)
            dense("appnp", [(d_x, hop_tab, C), (d_z, agg_tab, C)], [(d_o, x2_tab, C)])

            for n, (k, ph) in enumerate(((MAX1, "max1"), (MAX2, "max2"))):
                def load_edges(i, j, ch):
                    ge(sp, mixed, n * GROUPS + cnt(i, j) - GAP3[j] + 1)
                    if n == 0:
                        part = f_tab[bass.ds(i * (2 * R * GRP) + 2 * j * GRP, 2 * GRP), :].rearrange("(p q) c -> p (q c)", p=P)
                        sp.dma_start(part, zeros2[0]).then_inc(one["zeroed"], 16)
                    sp.dma_start(mix_r[S3[j]][C:P, :], t["edge_t"][:, bass.ds(i * (R * GRP) + j * GRP, GRP)]).then_inc(ld[j], 16)
                if n == 0:
                    sp.wait_ge(one["cleared"], 2)
                pipeline(sp, GI, [(0, load_edges)])
                sp.wait_ge(one["zeroed"], 16 * (TILES + 2 + GROUPS))
                barrier(sp, "sp")
                if n == 0:
                    dense("conv1", [(d_x, x2_tab, C), (d_z, agg_tab, C)], [(d_o, c1_tab, C)])
                else:
                    dense("conv2", [(d_x, c1_tab, C), (d_z, agg_tab, C), (d_w, x2_tab, C)], [(d_o, x3_tab, C), (d_u, u3_tab, C)])

            for dst, src in ((wt[0][0:C, :], t["cheb_w"]), (wb[0][0:C, :], t["cheb_b"]), (att[0][0:C, :], t["att_w"]),
                             (att_b[0][C:C + 1, :], t["att_b"].rearrange("(o c) -> o c", o=1)),
                             (fus[0][0:C, :], t["fus_w"]),
                             (bn[0][0:C, 4:5], t["bn_g"].rearrange("(c o) -> c o", o=1)),
                             (bn[0][0:C, 5:6], t["bn_b"].rearrange("(c o) -> c o", o=1))):
                sp.dma_start(dst, src).then_inc(one["prep_ld"], 16)
            barrier(sp, "sp")
            for n, ph in enumerate(("cheb1", "cheb2")):
                def store_cheb(i, j, ch):
                    sp.wait_ge(done, (HOPS - 1 + n) * GROUPS + cnt(i, j) + 1)
                    sp.dma_start(rows(p_slot, i, j, w=(n * C, n * C + C)), v3(cheb_a[j])).then_inc(wr[j], 16)
                    sp.dma_start(rows(q_tab[n], i, j), v3(cheb_b[j])).then_inc(wr[j], 16)
                with sp.Fori(0, GI) as i:
                    for j in range(R):
                        store_cheb(i, j, None)
                for j in range(R):
                    sp.wait_ge(wr[j], WR[ph] + 32 * GI)
                barrier(sp, "sp")

            def load_p(i, j, ch):
                ge(sp, fturned, 3 * (cnt(i, j) - GAP3[j] + 1))
                sp.dma_start(v3(cheb_p[S3[j]], 3 * C)[:, :, 0:2 * C], rows(p_slot, i, j)).then_inc(ld[j], 16)
            pipeline(sp, GI, [(0, load_p)])
            barrier(sp, "sp")

            dense("attend", [(a_x, x3_tab, C), (a_f, f_tab, FW)], [(a_h, h_tab, C)])
            barrier(sp, "sp")
            dense("norm", [(d_x, x3_tab, C), (d_z, h_tab, C)], [(d_o, t["out"], C)])

        @block.gpsimd
        def _(pl):
            ch = straight(pl, "pool")
            ch.step(nc.gpsimd.memset(ident[:, :], 0.0))
            ch.step(nc.gpsimd.affine_select(out=ident[:, :], in_=ident[:, :], compare_op=ALU.not_equal, fill=1.0,
                                            base=0, pattern=[[-1, P]], channel_multiplier=1))
            ch.step(nc.gpsimd.memset(tri[0], 1.0))
            ch.step(nc.gpsimd.affine_select(out=tri[0], in_=tri[0], compare_op=ALU.is_gt, fill=0.0,
                                            base=0, pattern=[[1, P]], channel_multiplier=-1))
            ch.step(nc.gpsimd.iota(iota_lo[0].bitcast(F16), [[1, GRP]], base=0, channel_multiplier=0, allow_small_or_imprecise_dtypes=True))
            ch.step(nc.gpsimd.iota(iota_hi[0].bitcast(F16), [[1, P]], base=0, channel_multiplier=0, allow_small_or_imprecise_dtypes=True))
            ch.step(nc.gpsimd.iota(deg[9][0:TILES, :], [[1, GRP]], base=0, channel_multiplier=GRP, allow_small_or_imprecise_dtypes=True))
            pl.sem_inc(one["idents"], 1)
            end_straight(ch, "pool")

            def gather(k, table, w):
                def f(i, j, ch=None):
                    pl.wait_ge(staged, k * GROUPS + cnt(i, j) + 1)
                    pl.sem_inc(pool_turn, 1)
                    for q in range(Q):
                        pl.indirect_dma_start(G[:, j, q * w:q * w + w], None, table,
                                              bass.IndirectOffsetOnAxis(ap=get_st[:, j, q:q + 1], axis=0)).then_inc(got[j], 16)
                return f

            def scatter(k, table, w, src):
                def f(i, j, ch=None):
                    if isinstance(k, int) and k == SUM0:
                        pl.wait_ge(one["zeroed"], 16 * TILES)
                    pl.wait_ge(put_ready, KU[k] * GROUPS + cnt(i, j) + 1)
                    pl.sem_inc(pool_turn, 1)
                    if k in OUTD:
                        pl.wait_ge(*((outdone, cnt(i, j) + 1) if k == HOPL else (fread, 4 * cnt(i, j) + 4)))
                    else:
                        pl.wait_ge(freed, scans(k) * GROUPS + cnt(i, j) + 1)
                    pl.sem_inc(pool_turn, 1)
                    for q in range(Q):
                        pl.indirect_dma_start(table, bass.IndirectOffsetOnAxis(ap=put_st[:, j, q:q + 1], axis=0),
                                              src[j][:, q * w:q * w + w], None, bounds_check=NP - 1, oob_is_err=False).then_inc(put[j], 16)
                return f

            def scatter_pass(k, table, w, to, tw, src):
                pipeline(pl, GI, [(0, gather(k, table, w)), (R, scatter(k, to, tw, src))])
                for j in range(R):
                    pl.wait_ge(put[j], PUT[k] + 64 * GI)
                barrier(pl, "pool")

            def gather_pass(k, table, w):
                f = gather(k, table, w)
                with pl.Fori(0, GI) as i:
                    for j in range(R):
                        f(i, j)

            scatter_pass(SUM0, t["x"], C, agg_tab, C, out_rows)
            barrier(pl, "pool")
            barrier(pl, "pool")
            gather_pass(DSTS, aug, TW)
            barrier(pl, "pool")
            gather_pass(HOP1, aug, TW)
            barrier(pl, "pool")
            with pl.Fori(0, ROUNDS) as r:
                gather_pass(r * 2 + HOP2, hop_tab, C)
                gather_pass(r * 2 + (HOP2 + 1), hop_tab, C)
            scatter_pass(HOPL, hop_tab, C, agg_tab, C, out_rows)
            barrier(pl, "pool")
            scatter_pass(MAX1, x2_tab, C, agg_tab, C, out_rows)
            barrier(pl, "pool")
            scatter_pass(MAX2, c1_tab, C, agg_tab, C, out_rows)
            barrier(pl, "pool")
            barrier(pl, "pool")
            gather_pass(CHEB1, u3_tab, C)
            barrier(pl, "pool")
            gather_pass(CHEB2, q_tab[0], C)
            barrier(pl, "pool")
            scatter_pass(CHEB3, q_tab[1], C, f_tab, FW, cheb_f)
            barrier(pl, "pool")
            barrier(pl, "pool")
            barrier(pl, "pool")

        @block.tensor
        def _(pe):
            def turn(k, extra=None, before=None, ring_=(pin, S3, GAP3)):
                banks, S, GAP = ring_

                def f(i, j, ch=None):
                    g = cnt(i, j)
                    if before is not None:
                        pe.wait_ge(before, g + 1)
                    ge(pe, got[j], 64 * (k * GI + i + 1))
                    if extra == "max":
                        ge(pe, moved, (k - MAX1 + 1) * GROUPS + g - GAP3[j] + 1)
                    else:
                        ge(pe, scanned, scans(k) * GROUPS + g - GAP[j] + 1)
                    w = TW if before is not None else C
                    for q in range(Q):
                        last = nc.tensor.transpose(banks[S[j]][0:C, q::Q], G[:, j, q * w:q * w + C], ident[:, :])
                    last.then_inc(taken, 1)
                return f

            def turn_back(k, ring_=(pout, S3, GAP3)):
                banks, S, GAP = ring_

                def f(i, j, ch=None):
                    g = scans(k) * GROUPS + cnt(i, j)
                    pe.wait_ge(scanned, g + 1)
                    ge(pe, freed, g - GAP[j] + 1)
                    for q in range(Q):
                        last = nc.tensor.transpose(banks[S[j]][:, q * C:q * C + C], sc[0:C, S3[j], q::Q], ident[0:C, 0:C])
                    last.then_inc(tout, 1)
                return f

            def hist(i, j, ch):
                pe.wait_ge(one["hot"], cnt(i, j) + 1)
                for q in range(Q):
                    row = onehot[q].bitcast(F16).rearrange("p (k n) -> p k n", k=2)
                    for k in range(2):
                        first = isinstance(i, int) and i == 0 and j == 0 and q == 0
                        last = nc.tensor.matmul(pmm[k][0:TILES, :], row[:, k, GRP:GRP + TILES], row[:, k, 0:GRP],
                                                start=first, stop=False, skip_group_check=True)
                last.then_inc(one["histed"], 1)

            pe.wait_ge(one["idents"], 1)
            pe.wait_ge(one["cleared"], 1)
            pipeline(pe, GI, [(0, turn(SUM0)), (0, hist), (0, turn_back(SUM0))])
            for k in range(2):
                nc.tensor.matmul(pmm[k][0:TILES, :], zeros[0].bitcast(F16)[:, 0:TILES], zeros[0].bitcast(F16)[:, 0:GRP],
                                 start=False, stop=True, skip_group_check=True)
            barrier(pe, "pe")
            pe.wait_ge(one["step_dve"], 1)
            nc.tensor.matmul(bank[0][0:TILES, 0:1], tri[0][0:TILES, 0:TILES], deg[2][0:TILES, GRP - 1:GRP],
                             start=True, stop=True).then_inc(one["step_pe"], 1)
            pe.wait_ge(one["step_dve"], 3)
            for n, d in enumerate((6, 7, 8)):
                for q in range(Q):
                    last = nc.tensor.transpose(bank[3 + n][:, q * TILES:(q + 1) * TILES], deg[d][0:TILES, q::Q], ident[0:TILES, 0:TILES])
            last.then_inc(one["step_pe"], 1)
            barrier(pe, "pe")

            def dturn(ph, src, ready, w=C, k=0):
                def f(i, j, ch):
                    if ready is None:
                        pe.wait_ge(ld[j], LD[ph] + 16 * nload[ph] * (i + 1))
                    else:
                        pe.wait_ge(dsem[ph, ready], cnt(i, j) + 1)
                    ge(pe, dsem[ph, "copied"], cnt(i, j) - GAP3[j] + 1)
                    for q in range(Q):
                        last = nc.tensor.transpose(pin[S3[j]][0:C, q * P:(q + 1) * P], src[j][:, q * C:q * C + C], ident[:, :])
                    last.then_inc(dsem[ph, "turned"], 1)
                return f

            def product(ph, lhs, weights, ready):
                def f(i, j, ch):
                    pe.wait_ge(dsem[ph, ready], cnt(i, j) + 1)
                    ge(pe, dsem[ph, "used"], cnt(i, j) - GAP2[j] + 1)
                    for q in range(Q):
                        last = nc.tensor.matmul(pmm[S2[j]][:, q * C:q * C + C], lhs[S3[j]][0:C + 1, q * P:(q + 1) * P], weights[0:C + 1, :],
                                                start=True, stop=True)
                    last.then_inc(dsem[ph, "mixed2"], 1)
                return f

            def gin_first(i, j, ch):
                pe.wait_ge(dsem["gin", "copied"], cnt(i, j) + 1)
                ge(pe, dsem["gin", "relued"], cnt(i, j) - GAP3[j] + 1)
                nc.tensor.matmul(pout[S3[j]][0:C, :], w_gin1[0][0:C, :], gin_r[S3[j]][0:C, :],
                                 start=True, stop=True).then_inc(dsem["gin", "mixed1"], 1)

            pe.wait_ge(setup_ld, 16 * 7)
            pipeline(pe, TI, [(0, dturn("gin", gin_z, "summed")), (1, gin_first), (2, product("gin", gin_h, w_gin2[0], "relued"))])
            barrier(pe, "pe")
            barrier(pe, "pe")

            def scan_pass(k, before=None):
                a, b = turn(k, before=before), turn_back(k)
                with pe.Fori(0, GI) as i:
                    for j in range(R):
                        a(i, j)
                        b(i, j)
            scan_pass(HOP1, before=moved)
            barrier(pe, "pe")
            with pe.Fori(0, ROUNDS) as r:
                scan_pass(r * 2 + HOP2)
                scan_pass(r * 2 + (HOP2 + 1))
            scan_pass(HOPL)
            barrier(pe, "pe")
            barrier(pe, "pe")

            pe.wait_ge(one["prep_ld"], 16 * 10)

            for n, (k, ph) in enumerate(((MAX1, "max1"), (MAX2, "max2"))):
                def mix(i, j, ch):
                    g = n * GROUPS + cnt(i, j)
                    pe.wait_ge(moved, GROUPS + g + 1)
                    pe.wait_ge(ld[j], LD[ph] + 16 * (i + 1))
                    ge(pe, scanned, scans(k) * GROUPS + cnt(i, j) - GAP2[j] + 1)
                    nc.tensor.matmul(pmm[S2[j]][0:C, :], w_mix[n], mix_r[S3[j]][:, :], start=True, stop=True).then_inc(mixed, 1)
                pipeline(pe, GI, [(0, turn(k, extra="max")), (0, mix), (0, turn_back(k))])
                barrier(pe, "pe")
                ph = f"conv{n + 1}"
                pipeline(pe, TI, [(0, dturn(ph, d_x, None)), (1, product(ph, d_t, w_root[n], "copied"))])
                barrier(pe, "pe")

            pe.wait_ge(one["step_dve"], 4)
            for n, (filt, col) in enumerate(FEATS):
                for m, kk in enumerate(filt):
                    rows_out = C + 1 if kk == 0 else C
                    lhs = wh[0][0:C, (filt_at[n] + m) * (C + 1):(filt_at[n] + m) * (C + 1) + rows_out]
                    nc.tensor.matmul(bank[kk][0:rows_out, col:col + C], lhs, fus[0][0:C, n * C:(n + 1) * C],
                                     start=True, stop=True, skip_group_check=True)
            for kk in range(4):
                who = [n for n, (filt, _) in enumerate(FEATS) if kk in filt]
                rows_out = C + 1 if kk == 0 else C
                for x, n in enumerate(who):
                    s0 = (filt_at[n] + kk) * (C + 1)
                    last = nc.tensor.matmul(bank[4 + kk][0:rows_out, 0:3], wh[0][0:C, s0:s0 + rows_out], att[0][0:C, n * 3:n * 3 + 3],
                                            start=(x == 0), stop=(x == len(who) - 1))
            last.then_inc(one["step_pe"], 1)
            barrier(pe, "pe")

            for k in (CHEB1, CHEB2):
                scan_pass(k)
                barrier(pe, "pe")

            def f_turn(i, j, ch):
                for n in range(3):
                    x = 3 * cnt(i, j) + n
                    if n == 2:
                        pe.wait_ge(thirds, cnt(i, j) + 1)
                    elif n == 0:
                        pe.wait_ge(ld[j], LD["cheb3"] + 16 * (i + 1))
                    ge(pe, fcopied, x - FGAP[n] + 1)
                    for q in range(Q):
                        at_ = q * 3 * C + n * C
                        last = nc.tensor.transpose(bank[FBANK[n]][0:C, q * P:(q + 1) * P],
                                                   cheb_p[S3[j]][:, at_:at_ + C], ident[:, :])
                    last.then_inc(fturned, 1)

            def f_mix(i, j, ch):
                pe.wait_ge(fcopied, 3 * cnt(i, j) + 3)
                for q in range(Q):
                    ge(pe, fread, 4 * cnt(i, j) + q - 1)
                    for n in range(3):
                        last = nc.tensor.matmul(bank[6 + q % 2][:, 0:WIDE[n + 1]], cheb_t[S2[j] * 3 + n][0:C, q * P:(q + 1) * P],
                                                w_feat[n + 1][0:C, 0:WIDE[n + 1]], start=(n == 0), stop=(n == 2), skip_group_check=True)
                    last.then_inc(fmixed, 1)
            pe.sem_inc(fmixed, FCREDIT)
            pipeline(pe, GI, [(0, turn(CHEB3, ring_=(bank[0:2], S2, GAP2))), (0, turn_back(CHEB3, ring_=(bank[2:4], S2, GAP2))),
                              (1, f_turn), (1, f_mix)])
            barrier(pe, "pe")

            def a_turn(i, j, ch):
                pe.wait_ge(ld[j], LD["attend"] + 32 * (i + 1))
                ge(pe, dsem["attend", "copied"], cnt(i, j) - GAP2[j] + 1)
                for q in range(Q):
                    last = nc.tensor.transpose(bank[S2[j]][0:C, q * P:(q + 1) * P], a_x[j][:, q * C:q * C + C], ident[:, :])
                last.then_inc(dsem["attend", "turned"], 1)

            def a_mix(i, j, ch):
                pe.wait_ge(one["ones_set"], 3)
                pe.wait_ge(dsem["attend", "copied"], cnt(i, j) + 1)
                for q in range(Q):
                    if q % 2 == 0:
                        ge(pe, dsem["attend", "summed"], 2 * cnt(i, j) + q // 2 - 1)
                    last = nc.tensor.matmul(bank[2 + q][:, 0:FW], a_t[S3[j]][0:C + 1, q * P:(q + 1) * P], w_feat[0][0:C + 1, :],
                                            start=True, stop=True)
                    if q % 2:
                        last.then_inc(dsem["attend", "mixed2"], 1)

            def a_back(i, j, ch):
                pe.wait_ge(dsem["attend", "used"], cnt(i, j) + 1)
                ge(pe, dsem["attend", "final"], cnt(i, j) - GAP2[j] + 1)
                for q in range(Q):
                    last = nc.tensor.transpose(pmm[S2[j]][0:C, q * P:(q + 1) * P], a_h[j][:, q * C:q * C + C], ident[:, :])
                last.then_inc(dsem["attend", "turned2"], 1)
            pipeline(pe, TI, [(0, a_turn), (1, a_mix), (4, a_back)])
            barrier(pe, "pe")
            pe.wait_ge(one["step_dve"], 6)
            for n in range(2):
                last = nc.tensor.matmul(bank[0][:, n * C:(n + 1) * C], bn_wide[n][0:C, :], ident[0:C, 0:C], start=True, stop=True)
            last.then_inc(one["step_pe"], 1)
            barrier(pe, "pe")
            barrier(pe, "pe")

        @block.scalar
        def _(act):
            def stage(k, idx):
                def f(i, j, ch=None):
                    ge(act, taken, k * GROUPS + cnt(i, j) - R + 1)
                    nc.scalar.copy(get_st[:, j, :], idx[:, at(i, j, Q)]).then_inc(staged, 1)
                return f

            def finish(k, evacuate=True):
                def f(i, j, ch=None):
                    ge(act, put[j], PUT[k] + 64 * i)
                    nc.scalar.copy(put_st[:, j, :], put_i[:, at(i, j, Q)]).then_inc(put_ready, 1)
                    if evacuate:
                        act.wait_ge(tout, scans(k) * GROUPS + cnt(i, j) + 1)
                        nc.scalar.copy(out_r[:, j, :], pout[S3[j]][:, 0:QC]).then_inc(freed, 1)
                return f

            def stage_pass(k, idx):
                f = stage(k, idx)
                with act.Fori(0, GI) as i:
                    for j in range(R):
                        f(i, j)

            act.wait_ge(one["cleared"], 1)
            with act.Fori(0, TI) as i:
                for j in range(R):
                    act.dma_start(rows(agg_tab, i, j), v3(zeros[0][:, 0:QC])).then_inc(one["zeroed"], 16)
            act.wait_ge(setup_ld, 16 * 7)
            act.wait_ge(one["puts"], 1)
            pipeline(act, GI, [(0, stage(SUM0, src_i)), (R, finish(SUM0))])
            barrier(act, "act")
            act.wait_ge(one["step_dve"], 2)
            nc.scalar.activation(deg[7][0:TILES, :], deg[7][0:TILES, :], ACT.Sqrt).then_inc(one["step_act"], 1)
            nc.scalar.activation(deg[8][0:TILES, :], deg[8][0:TILES, :], ACT.Sqrt).then_inc(one["step_act"], 1)
            barrier(act, "act")

            def copied(ph, dst):
                def f(i, j, ch):
                    act.wait_ge(dsem[ph, "turned"], cnt(i, j) + 1)
                    ge(act, dsem[ph, "mixed1" if ph == "gin" else "mixed2"], cnt(i, j) - GAP3[j] + 1)
                    nc.scalar.copy(dst[S3[j]][0:C, :], pin[S3[j]][0:C, :]).then_inc(dsem[ph, "copied"], 1)
                return f

            def squares(ph, src, sq):
                def f(i, j, ch):
                    act.wait_ge(dsem[ph, "centred"], cnt(i, j) + 1)
                    ge(act, dsem[ph, "reduced"], cnt(i, j) - GAP3[j] + 1)
                    nc.scalar.activation(sq[S3[j]], src[j], ACT.Square).then_inc(dsem[ph, "squared"], 1)
                return f

            def roots(ph, s):
                def f(i, j, ch):
                    act.wait_ge(dsem[ph, "reduced"], cnt(i, j) + 1)
                    nc.scalar.activation(s[j][:, 3 * Q:4 * Q], s[j][:, 2 * Q:3 * Q], ACT.Sqrt, bias=eps_col[:, :], scale=1.0 / C).then_inc(dsem[ph, "rooted"], 1)
                return f

            def gin_relu(i, j, ch):
                act.wait_ge(dsem["gin", "mixed1"], cnt(i, j) + 1)
                ge(act, dsem["gin", "mixed2"], cnt(i, j) - GAP3[j] + 1)
                nc.scalar.activation(gin_h[S3[j]][0:C, :], pout[S3[j]][0:C, :], ACT.Relu, bias=b_gin1[0][0:C, :]).then_inc(dsem["gin", "relued"], 1)

            pipeline(act, TI, [(0, copied("gin", gin_r)), (1, gin_relu), (3, squares("gin", gin_y, gin_sq)), (4, roots("gin", gin_s))])
            barrier(act, "act")
            stage_pass(DSTS, dst_i)
            barrier(act, "act")
            stage_pass(HOP1, src_i)
            barrier(act, "act")
            with act.Fori(0, ROUNDS) as r:
                for h in range(2):
                    act.wait_ge(table_written, r * 2 + (h + 1))
                    stage_pass(r * 2 + (HOP2 + h), hop_i[h])
            act.wait_ge(table_written, HOPS - 1)
            pipeline(act, GI, [(0, stage(HOPL, hop_i[0])), (R, finish(HOPL, evacuate=False))])
            barrier(act, "act")
            pipeline(act, TI, [(0, squares("appnp", d_y, d_sq)), (1, roots("appnp", d_s))])
            barrier(act, "act")
            for n, k in enumerate((MAX1, MAX2)):
                pipeline(act, GI, [(0, stage(k, src_i)), (R, finish(k))])
                barrier(act, "act")
                ph = f"conv{n + 1}"
                tail = [(2, squares(ph, d_y, d_sq)), (3, roots(ph, d_s))] if n else []
                pipeline(act, TI, [(0, copied(ph, d_t))] + tail)
                barrier(act, "act")
            barrier(act, "act")
            stage_pass(CHEB1, src_i)
            barrier(act, "act")
            stage_pass(CHEB2, q_i)
            barrier(act, "act")

            def f_copied(i, j, ch):
                for n in range(3):
                    act.wait_ge(fturned, 3 * cnt(i, j) + n + 1)
                    act.wait_ge(fmixed, FCREDIT + 4 * (cnt(i, j) - GAP2[j] + 1))
                    nc.scalar.copy(cheb_t[S2[j] * 3 + n][0:C, :], bank[FBANK[n]][0:C, :]).then_inc(fcopied, 1)
            pipeline(act, GI, [(0, stage(CHEB3, q_i)), (R, finish(CHEB3, evacuate=False)), (R - 1, f_copied)])
            barrier(act, "act")

            def a_copied(i, j, ch):
                act.wait_ge(dsem["attend", "turned"], cnt(i, j) + 1)
                ge(act, dsem["attend", "mixed2"], 2 * (cnt(i, j) - GAP3[j] + 1))
                nc.scalar.copy(a_t[S3[j]][0:C, :], bank[S2[j]][0:C, :]).then_inc(dsem["attend", "copied"], 1)

            def a_scaled(i, j, ch):
                act.wait_ge(dsem["attend", "scaled"], cnt(i, j) + 1)
                ge(act, st[j], ST["attend"] + 16 * i)
                for q in range(Q):
                    e = a_s[j][:, Q + 3 * q + 2:Q + 3 * q + 3]
                    ins = nc.scalar.activation(a_h[j][:, q * C:q * C + C], a_f[j][:, q * FW:q * FW + C], ACT.Copy, scale=e)
                ins.then_inc(dsem["attend", "shared"], 1)

            def a_exp(i, j, ch):
                act.wait_ge(dsem["attend", "topped"], cnt(i, j) + 1)
                nc.scalar.activation(a_s[j][:, Q:4 * Q], a_s[j][:, Q:4 * Q], ACT.Exp).then_inc(dsem["attend", "raised"], 1)
            pipeline(act, TI, [(0, a_copied), (1, a_exp), (2, a_scaled)])
            barrier(act, "act")
            act.wait_ge(one["step_dve"], 5)
            nc.scalar.activation(bn[0][0:C, 2:3], bn[0][0:C, 1:2], ACT.Sqrt, bias=eps_col[0:C, :]).then_inc(one["step_act"], 1)
            barrier(act, "act")
            pipeline(act, TI, [(0, squares("norm", d_y, d_sq)), (1, roots("norm", d_s))])
            barrier(act, "act")

        @block.vector
        def _(dve):
            V = nc.vector
            ch = straight(dve, "dve")
            V.memset(zeros[0], 0.0)
            V.memset(eps_col[:, :], EPS)
            V.memset(gin_h[0][C:C + 1, :], 1.0)
            V.memset(gin_h[1][C:C + 1, :], 1.0)
            V.memset(gin_h[2][C:C + 1, :], 1.0)
            for j in range(R):
                V.memset(gin_a[j], 0.0)
            ch.step(V.memset(sc[:, :, :], 0.0))
            dve.sem_inc(one["cleared"], 1)
            dve.wait_ge(setup_ld, 16 * 7)
            flag = tmp[:, 0, 0:IDX]
            digit = tmp[:, 1, 0:IDX].bitcast(I32)
            ch.step(V.tensor_tensor(flag, dst_i[:, :], put_i[:, :], ALU.is_equal))
            ch.step(V.scalar_tensor_tensor(put_i[:, :], flag, float(FAR), dst_i[:, :], ALU.mult, ALU.add))
            dve.sem_inc(one["puts"], 1)
            for n, a in enumerate((src_i, dst_i)):
                ch.step(V.tensor_scalar(digit, a[:, :], GRP - 1, None, ALU.bitwise_and))
                ch.step(V.tensor_copy(lo_hi[:, 2 * n, :], digit))
                ch.step(V.tensor_scalar(digit, a[:, :], GRP.bit_length() - 1, None, ALU.logical_shift_right))
                ch.step(V.tensor_copy(lo_hi[:, 2 * n + 1, :], digit))
            end_straight(ch, "dve")
            dve.wait_ge(one["idents"], 1)

            def keep_flags(i, j, ch):
                dve.wait_ge(ld[j], LD["keep"] + 16 * (i + 1))
                row = keep_ld[j].bitcast(I32)
                V.tensor_tensor(keep[0:C, at(i, j, GRP)], row[0:C, 1:GRP + 1], row[0:C, 0:GRP], ALU.is_equal).then_inc(keeps, 1)

            def onehots(i, j, ch):
                ge(dve, one["histed"], cnt(i, j))
                for q in range(Q):
                    row = onehot[q].bitcast(F16).rearrange("p (k n) -> p k n", k=2)
                    for n in range(2):
                        V.tensor_scalar(row[:, n, 0:GRP], iota_lo[0].bitcast(F16), lo_hi[:, 2 * n, at(i, j, Q, 1, q)], None, ALU.is_equal)
                        last = V.tensor_scalar(row[:, n, GRP:GRP + P], iota_hi[0].bitcast(F16), lo_hi[:, 2 * n + 1, at(i, j, Q, 1, q)], None, ALU.is_equal)
                last.then_inc(one["hot"], 1)

            def scan(k, mask=None, banks=pin, S=S3):

                def f(i, j, ch=None):
                    g = scans(k) * GROUPS + cnt(i, j)
                    if mask is None:
                        dve.wait_ge(taken, k * GROUPS + cnt(i, j) + 1)
                        src, m, ops = banks[S[j]][0:C, :], keep[0:C, at(i, j, GRP)], (ALU.mult, ALU.add)
                    else:
                        dve.wait_ge(mixed, (k - MAX1) * GROUPS + cnt(i, j) + 1)
                        src, m, ops = pmm[S2[j]][0:C, :], mask[0:C, at(i, j, GRP)], (ALU.add, ALU.max)
                    if isinstance(k, int) and k == SUM0:
                        dve.wait_ge(keeps, cnt(i, j) + 1)
                    ge(dve, tout, g - GAP3[j] + 1)
                    ge(dve, scanned, g)
                    V.tensor_tensor_scan(sc[0:C, S3[j], :], m, src, sc[0:C, S3[j - 1], GRP - 1:GRP], *ops).then_inc(scanned, 1)
                return f

            pipeline(dve, GI, [(0, keep_flags), (0, onehots), (0, scan(SUM0))])
            barrier(dve, "dve")

            ch = straight(dve, "dve")
            D = [d[0:TILES, :] for d in deg]
            h_out, h_in, cum, one_, off, f_in, slot_map, s_in, s_out, node = D
            V.memset(one_, 1.0)
            V.tensor_copy(h_out, pmm[0][0:TILES, :])
            ch.step(V.tensor_copy(h_in, pmm[1][0:TILES, :]))
            ch.step(V.tensor_tensor_scan(cum, one_, h_in, 0.0, ALU.mult, ALU.add))
            dve.sem_inc(one["step_dve"], 1)
            V.tensor_scalar(f_in, h_in, 1.0, None, ALU.min)
            V.tensor_scalar(s_in, h_in, 1.0, None, ALU.add)
            V.tensor_scalar(s_out, h_out, 1.0, None, ALU.max)
            ch.step(V.tensor_scalar(h_out, h_out, 1.0, None, ALU.min))
            dve.wait_ge(one["step_pe"], 1)
            ch.step(V.tensor_copy(off[:, 0:1], bank[0][0:TILES, 0:1]))
            ch.step(V.tensor_scalar(slot_map, cum, off[:, 0:1], float(NP - 1), ALU.add, ALU.add))
            ch.step(V.tensor_tensor(slot_map, slot_map, node, ALU.subtract))
            ch.step(V.tensor_tensor(slot_map, slot_map, f_in, ALU.mult))
            ch.step(V.tensor_tensor(slot_map, slot_map, node, ALU.add))
            dve.sem_inc(one["step_dve"], 1)
            dve.wait_ge(one["step_act"], 2)
            ch.step(V.reciprocal(s_in, s_in))
            ch.step(V.reciprocal(s_out, s_out))
            ch.step(V.tensor_tensor(s_out, s_out, h_out, ALU.mult))
            dve.sem_inc(one["step_dve"], 1)
            dve.wait_ge(one["step_pe"], 2)
            for n in range(3):
                last = V.tensor_copy(node_sc[:, n, :].rearrange("p (t q) -> p q t", q=Q),
                                     bank[3 + n][:, 0:Q * TILES].rearrange("p (q t) -> p q t", q=Q))
            ch.step(last)
            end_straight(ch, "dve")
            barrier(dve, "dve")

            def centre(ph, y, s, ch, j, sem_):
                ch.step(V.tensor_reduce(s[j][:, 0:Q], v3(y[j]), AX.X, ALU.add))
                ch.step(V.tensor_scalar(s[j][:, Q:2 * Q], s[j][:, 0:Q], -1.0 / C, None, ALU.mult))
                V.tensor_tensor(v3(y[j]), v3(y[j]), spread(s[j][:, Q:2 * Q]), ALU.add).then_inc(dsem[ph, "centred"], 1)

            def reduce(ph, sq, s):
                def f(i, j, ch):
                    dve.wait_ge(dsem[ph, "squared"], cnt(i, j) + 1)
                    V.tensor_reduce(s[j][:, 2 * Q:3 * Q], v3(sq[S3[j]]), AX.X, ALU.add).then_inc(dsem[ph, "reduced"], 1)
                return f

            def scaled(ph, y, s, ch, i, j, out, nst):
                dve.wait_ge(dsem[ph, "rooted"], cnt(i, j) + 1)
                ch.step(V.reciprocal(s[j][:, 0:Q], s[j][:, 3 * Q:4 * Q]))
                ge(dve, st[j], ST[ph] + 16 * nst * i)
                return V.tensor_tensor(v3(out[j]), v3(y[j]), spread(s[j][:, 0:Q]), ALU.mult)

            def gin_sum(i, j, ch):
                dve.wait_ge(ld[j], LD["gin"] + 32 * (i + 1))
                V.tensor_tensor(gin_z[j], gin_z[j], gin_x[j], ALU.add).then_inc(dsem["gin", "summed"], 1)

            def gin_res(i, j, ch):
                dve.wait_ge(dsem["gin", "mixed2"], cnt(i, j) + 1)
                V.tensor_tensor(gin_y[j], pmm[S2[j]][:, 0:QC], gin_x[j], ALU.add).then_inc(dsem["gin", "used"], 1)
                dve.wait_ge(dsem["gin", "used"], cnt(i, j) + 1)
                centre("gin", gin_y, gin_s, ch, j, None)

            def gin_out(i, j, ch):
                ch.step(scaled("gin", gin_y, gin_s, ch, i, j, gin_o, 2))
                row = v3(gin_a[j], TW)
                sc_ = node_sc[:, :, at(i, j, Q)]
                V.tensor_copy(row[:, :, C:C + 3], sc_.rearrange("p k q -> p q k"))
                V.tensor_tensor(row[:, :, 0:C], v3(gin_o[j]), spread(sc_[:, 1, :]), ALU.mult).then_inc(dsem["gin", "final"], 1)
            pipeline(dve, TI, [(0, gin_sum), (3, gin_res), (4, reduce("gin", gin_sq, gin_s)), (5, gin_out)], "dve", steps=R * 4)
            barrier(dve, "dve")

            def dst_rows(i, j):
                dve.wait_ge(got[j], 64 * (DSTS * GI + i + 1))
                row = v3(G[:, j, :], TW)
                V.tensor_copy(sd_in[:, at(i, j, Q)], row[:, :, C + 1])
                V.tensor_copy(w_out[:, at(i, j, Q)], row[:, :, C + 2])
                V.tensor_copy(v3(g0[:, at(i, j, QC)]), row[:, :, 0:C]).then_inc(taken, 1)
            with dve.Fori(0, GI) as i:
                for j in range(R):
                    dst_rows(i, j)
            ch = straight(dve, "dve")
            dve.wait_ge(taken, (DSTS + 1) * GROUPS)
            ch.step(V.tensor_tensor(w_hop[:, :], sd_in[:, :], sd_in[:, :], ALU.mult))
            ch.step(V.tensor_scalar(w_hop[:, :], w_hop[:, :], KEEP, None, ALU.mult))
            ch.step(V.reciprocal(sd_in[:, :], sd_in[:, :]))
            end_straight(ch, "dve")
            barrier(dve, "dve")

            def hop(k, h, old, last=False):
                sc_f = scan(k)

                def f(i, j, ch):
                    g = scans(k) * GROUPS + cnt(i, j)
                    if old is g0:
                        ge(dve, got[j], 64 * (HOP1 * GI + i + 1))
                        V.tensor_copy(hop_i[0][:, at(i, j, Q)], v3(G[:, j, :], TW)[:, :, C]).then_inc(moved, 1)
                    sc_f(i, j)
                    dve.wait_ge(tout, g + 1)
                    a, b = tmp[:, j % 2, :], at(i, j, QC)
                    V.tensor_tensor(a, pout[S3[j]][:, 0:QC], old[:, b], ALU.add).then_inc(freed, 1)
                    dve.wait_ge(freed, g + 1)
                    ch.step(V.tensor_tensor(v3(a), v3(a), spread(w_hop[:, at(i, j, Q)]), ALU.mult))
                    if not last:
                        V.scalar_tensor_tensor(state[:, b], g0[:, b], ALPHA, a, ALU.mult, ALU.add).then_inc(done, 1)
                    else:
                        ch.step(V.scalar_tensor_tensor(a, g0[:, b], ALPHA - 1.0, a, ALU.mult, ALU.add))
                        dve.wait_ge(put_ready, KU[HOPL] * GROUPS + cnt(i, j) + 1)
                        V.tensor_tensor(v3(out_r[:, j, :]), v3(a), spread(sd_in[:, at(i, j, Q)]), ALU.mult).then_inc(outdone, 1)
                return f

            def hop_pass(k, old, start, steps=R, last=False):
                f = hop(k, None, old, last)
                with dve.Fori(0, GI) as i:
                    ch = Chain(dve, "dve", start + i * steps)
                    for j in range(R):
                        f(i, j, ch)
                    assert ch.n == steps
            hop_pass(HOP1, g0, chain_at["dve"])
            chain_at["dve"] += R * GI
            ch = straight(dve, "dve")
            dve.wait_ge(moved, GROUPS)
            dve.wait_ge(done, GROUPS)
            ch.step(V.tensor_scalar(flag, hop_i[0][:, :], float(NP), None, ALU.is_ge))
            ch.step(V.scalar_tensor_tensor(hop_i[1][:, :], flag, float(EP), hop_i[0][:, :], ALU.mult, ALU.add))
            ch.step(V.tensor_scalar(digit, hop_i[0][:, :], float(NP + EP), None, ALU.subtract))
            ch.step(V.tensor_tensor(digit, digit, flag, ALU.mult))
            ch.step(V.tensor_scalar(q_i[:, :], digit, float(EP), None, ALU.add))
            end_straight(ch, "dve")
            barrier(dve, "dve")
            with dve.Fori(0, ROUNDS) as r:
                for h in range(2):
                    hop_pass(r * 2 + (HOP2 + h), state, r * (2 * R * GI) + (chain_at["dve"] + h * R * GI))
            chain_at["dve"] += ROUNDS * 2 * R * GI
            hop_pass(HOPL, state, chain_at["dve"], steps=2 * R, last=True)
            chain_at["dve"] += 2 * R * GI
            barrier(dve, "dve")

            def appnp_res(i, j, ch):
                dve.wait_ge(ld[j], LD["appnp"] + 32 * (i + 1))
                V.scalar_tensor_tensor(d_y[j], d_x[j], 2.0, d_z[j], ALU.mult, ALU.add).then_inc(dsem["appnp", "used"], 1)
                dve.wait_ge(dsem["appnp", "used"], cnt(i, j) + 1)
                centre("appnp", d_y, d_s, ch, j, None)

            def ln_out(ph, nst):
                def f(i, j, ch):
                    scaled(ph, d_y, d_s, ch, i, j, d_o, nst).then_inc(dsem[ph, "final"], 1)
                return f
            V.memset(d_t[0][C:C + 1, :], 1.0)
            V.memset(d_t[1][C:C + 1, :], 1.0)
            V.memset(d_t[2][C:C + 1, :], 1.0)
            pipeline(dve, TI, [(0, appnp_res), (1, reduce("appnp", d_sq, d_s)), (2, ln_out("appnp", 1))], "dve", steps=R * 3)
            ch = straight(dve, "dve")
            ch.step(V.tensor_scalar(neg[0:C, :], keep[0:C, :], 1.0, BIG, ALU.subtract, ALU.mult))
            end_straight(ch, "dve")
            barrier(dve, "dve")
            ch = straight(dve, "dve")
            ch.step(V.memset(zeros2[0], 0.0))
            end_straight(ch, "dve")
            dve.sem_inc(one["cleared"], 1)

            for n, k in enumerate((MAX1, MAX2)):
                def move(i, j, ch):
                    g = n * GROUPS + cnt(i, j)
                    dve.wait_ge(taken, k * GROUPS + cnt(i, j) + 1)
                    ge(dve, mixed, g - GAP3[j] + 1)
                    V.tensor_copy(mix_r[S3[j]][0:C, :], pin[S3[j]][0:C, :]).then_inc(moved, 1)
                pipeline(dve, GI, [(0, move), (0, scan(k, mask=neg))])
                barrier(dve, "dve")

                ph = f"conv{n + 1}"

                def conv_res(i, j, ch):
                    dve.wait_ge(dsem[ph, "mixed2"], cnt(i, j) + 1)
                    dve.wait_ge(ld[j], LD[ph] + 16 * nload[ph] * (i + 1))
                    if n:
                        a = d_y[j]
                        ch.step(V.tensor_tensor(a, pmm[S2[j]][:, 0:QC], d_z[j], ALU.add))
                        ch.step(V.scalar_tensor_tensor(a, a, 0.01, a, ALU.mult, ALU.max))
                        V.tensor_tensor(a, a, d_w[j], ALU.add).then_inc(dsem[ph, "used"], 1)
                        dve.wait_ge(dsem[ph, "used"], cnt(i, j) + 1)
                        centre(ph, d_y, d_s, ch, j, None)
                    else:
                        V.tensor_tensor(d_y[j], pmm[S2[j]][:, 0:QC], d_z[j], ALU.add).then_inc(dsem[ph, "used"], 1)
                        dve.wait_ge(dsem[ph, "used"], cnt(i, j) + 1)
                        ge(dve, st[j], ST[ph] + 16 * i)
                        V.scalar_tensor_tensor(d_o[j], d_y[j], 0.01, d_y[j], ALU.mult, ALU.max).then_inc(dsem[ph, "final"], 1)

                def conv_out(i, j, ch):
                    ch.step(scaled(ph, d_y, d_s, ch, i, j, d_o, 2))
                    V.tensor_tensor(v3(d_u[j]), v3(d_o[j]), spread(out_sc_[0][:, at(i, j, Q)]), ALU.mult).then_inc(dsem[ph, "final"], 1)
                if n:
                    pipeline(dve, TI, [(1, conv_res), (2, reduce(ph, d_sq, d_s)), (3, conv_out)], "dve", steps=R * 6)
                else:
                    pipeline(dve, TI, [(1, conv_res)])
                barrier(dve, "dve")

            ch = straight(dve, "dve")
            dve.wait_ge(one["prep_ld"], 16 * 17)
            W = lambda n, m: wt[0][0:C, (filt_at[n] + m) * C:(filt_at[n] + m + 1) * C]
            H = lambda n, m: wh[0][0:C, (filt_at[n] + m) * (C + 1):(filt_at[n] + m) * (C + 1) + C]
            V.tensor_copy(H(0, 0), W(0, 0))
            V.tensor_scalar(H(0, 1), W(0, 1), -1.0, None, ALU.mult)
            V.tensor_tensor(H(1, 0), W(1, 0), W(1, 2), ALU.subtract)
            V.tensor_scalar(H(1, 1), W(1, 1), -1.0, None, ALU.mult)
            V.tensor_scalar(H(1, 2), W(1, 2), 2.0, None, ALU.mult)
            V.tensor_tensor(H(2, 0), W(2, 0), W(2, 2), ALU.subtract)
            V.tensor_tensor(H(2, 1), W(2, 3), W(2, 1), ALU.subtract)
            V.tensor_scalar(H(2, 2), W(2, 2), 2.0, None, ALU.mult)
            V.tensor_scalar(H(2, 3), W(2, 3), 2.0, None, ALU.mult)
            for n in range(3):
                c = filt_at[n] * (C + 1) + C
                last = V.tensor_copy(wh[0][0:C, c:c + 1], wb[0][0:C, n:n + 1])
            ch.step(last)
            dve.sem_inc(one["step_dve"], 1)
            dve.wait_ge(one["step_pe"], 3)
            for kk in range(4):
                kr = C + 1 if kk == 0 else C
                V.tensor_copy(w_feat[kk][0:kr, LOGIT:LOGIT + 3], bank[4 + kk][0:kr, 0:3])
                V.tensor_copy(w_feat[kk][0:kr, 0:C], bank[kk][0:kr, 0:C])
                if WIDE[kk] > C + 3:
                    ch.step(V.tensor_copy(w_feat[kk][0:kr, C + 3:WIDE[kk]], bank[kk][0:kr, C + 3:WIDE[kk]]))
            ch.step(V.tensor_tensor(w_feat[0][C:C + 1, :], w_feat[0][C:C + 1, :], att_b[0][C:C + 1, :], ALU.add))
            end_straight(ch, "dve")
            barrier(dve, "dve")
            for n, k in enumerate((CHEB1, CHEB2)):
                sc_f = scan(k)

                def cheb(i, j, ch):
                    g = scans(k) * GROUPS + cnt(i, j)
                    sc_f(i, j)
                    dve.wait_ge(tout, g + 1)
                    ge(dve, wr[j], WR["cheb1" if n == 0 else "cheb2"] + 32 * i)
                    w = spread(w_out[:, at(i, j, Q)])
                    V.tensor_tensor(v3(cheb_a[j]), v3(pout[S3[j]][:, 0:QC]), w, ALU.mult).then_inc(freed, 1)
                    dve.wait_ge(freed, g + 1)
                    V.tensor_tensor(v3(cheb_b[j]), v3(cheb_a[j]), w, ALU.mult).then_inc(done, 1)
                with dve.Fori(0, GI) as i:
                    for j in range(R):
                        cheb(i, j, None)
                barrier(dve, "dve")


            def cheb_last(i, j, ch):
                g = scans(CHEB3) * GROUPS + cnt(i, j)
                dve.wait_ge(tout, g + 1)
                a, b = tmp[:, j % 2, :], v3(cheb_p[S3[j]], 3 * C)
                V.tensor_tensor(v3(a), v3(bank[2 + S2[j]][:, 0:QC]), spread(w_out[:, at(i, j, Q)]), ALU.mult).then_inc(freed, 1)
                dve.wait_ge(freed, g + 1)
                dve.wait_ge(ld[j], LD["cheb3"] + 16 * (i + 1))
                V.scalar_tensor_tensor(b[:, :, 2 * C:3 * C], v3(a), -2.0, b[:, :, 0:C], ALU.mult, ALU.add).then_inc(thirds, 1)

            def f_rows(i, j, ch):
                dve.wait_ge(put_ready, KU[CHEB3] * GROUPS + cnt(i, j) + 1)
                for q in range(Q):
                    dve.wait_ge(fmixed, FCREDIT + 4 * cnt(i, j) + q + 1)
                    V.tensor_copy(cheb_f[j][:, q * FW:(q + 1) * FW], bank[6 + q % 2][:, 0:FW]).then_inc(fread, 1)
            pipeline(dve, GI, [(0, scan(CHEB3, banks=bank[0:2], S=S2)), (0, cheb_last), (1, f_rows)])
            barrier(dve, "dve")
            for s_ in range(3):
                V.memset(a_t[s_][C:C + 1, :], 1.0).then_inc(one["ones_set"], 1)

            wide = ps[:, 2:2 + Q, :]

            def a_sum(i, j, ch):
                s_, f_ = a_s[j], v3(a_f[j], FW)
                logit = f_[:, :, LOGIT:LOGIT + 3]
                e3 = s_[:, Q:4 * Q].rearrange("p (q k) -> p q k", k=3)
                for n in range(2):
                    half = slice(2 * n, 2 * n + 2)
                    dve.wait_ge(dsem["attend", "mixed2"], 2 * cnt(i, j) + n + 1)
                    V.tensor_tensor(f_[:, half, :], wide[:, half, 0:FW], f_[:, half, :], ALU.add).then_inc(dsem["attend", "summed"], 1)
                dve.wait_ge(dsem["attend", "summed"], 2 * cnt(i, j) + 2)
                ch.step(V.tensor_reduce(s_[:, 0:Q], logit, AX.X, ALU.max))
                V.tensor_tensor(e3, logit, s_[:, 0:Q].unsqueeze(2).to_broadcast([P, Q, 3]), ALU.subtract).then_inc(dsem["attend", "topped"], 1)

            def a_soft(i, j, ch):
                s_ = a_s[j]
                e3 = s_[:, Q:4 * Q].rearrange("p (q k) -> p q k", k=3)
                dve.wait_ge(dsem["attend", "raised"], cnt(i, j) + 1)
                ch.step(V.tensor_reduce(s_[:, 4 * Q:5 * Q], e3, AX.X, ALU.add))
                ch.step(V.reciprocal(s_[:, 4 * Q:5 * Q], s_[:, 4 * Q:5 * Q]))
                V.tensor_tensor(e3, e3, s_[:, 4 * Q:5 * Q].unsqueeze(2).to_broadcast([P, Q, 3]), ALU.mult).then_inc(dsem["attend", "scaled"], 1)

            def a_fuse(i, j, ch):
                dve.wait_ge(dsem["attend", "shared"], cnt(i, j) + 1)
                f_ = v3(a_f[j], FW)
                for n in (1, 0):
                    col = FEATS[n][1]
                    for q in range(Q):
                        h, e = a_h[j][:, q * C:q * C + C], a_s[j][:, Q + 3 * q + n:Q + 3 * q + n + 1]
                        ins = V.scalar_tensor_tensor(h, f_[:, q, col:col + C], e, h, ALU.mult, ALU.add)
                    if n:
                        ch.step(ins)
                ins.then_inc(dsem["attend", "used"], 1)

            def a_stats(i, j, ch):
                dve.wait_ge(dsem["attend", "turned2"], cnt(i, j) + 1)
                V.bn_stats(stats[0][0:C, at(i, j, 6)], pmm[S2[j]][0:C, :]).then_inc(dsem["attend", "final"], 1)
            pipeline(dve, TI, [(1, a_sum), (2, a_soft), (3, a_fuse), (5, a_stats)], "dve", steps=R * 4)
            ch = straight(dve, "dve")
            real = (N - (TILES - 1) * GRP) // Q
            dve.wait_ge(dsem["attend", "final"], TILES)
            ch.step(V.bn_stats(stats[0][0:C, (TILES - 1) * 6:TILES * 6], pmm[S2[R - 1]][0:C, :].rearrange("c (q p) -> c q p", q=Q)[:, :, 0:real]))
            end_straight(ch, "dve")
            barrier(dve, "dve")
            ch = straight(dve, "dve")
            b_ = bn[0][0:C, :]
            ch.step(V.bn_aggr(b_[:, 0:2], stats[0][0:C, :]))
            dve.sem_inc(one["step_dve"], 1)
            dve.wait_ge(one["step_act"], 3)
            ch.step(V.reciprocal(b_[:, 3:4], b_[:, 2:3]))
            ch.step(V.tensor_tensor(b_[:, 6:7], b_[:, 3:4], b_[:, 4:5], ALU.mult))
            ch.step(V.tensor_tensor(b_[:, 7:8], b_[:, 0:1], b_[:, 6:7], ALU.mult))
            ch.step(V.tensor_tensor(b_[:, 7:8], b_[:, 5:6], b_[:, 7:8], ALU.subtract))
            V.tensor_copy(bn_wide[0][0:C, :], b_[:, 6:7].to_broadcast([C, P]))
            ch.step(V.tensor_copy(bn_wide[1][0:C, :], b_[:, 7:8].to_broadcast([C, P])))
            dve.sem_inc(one["step_dve"], 1)
            dve.wait_ge(one["step_pe"], 4)
            ch.step(V.tensor_copy(bn_row[0], bank[0][:, 0:2 * C]))
            end_straight(ch, "dve")
            barrier(dve, "dve")

            def norm_res(i, j, ch):
                dve.wait_ge(ld[j], LD["norm"] + 32 * (i + 1))
                y = v3(d_y[j])
                row = lambda a: bn_row[0][:, a:a + C].unsqueeze(1).to_broadcast([P, Q, C])
                ch.step(V.tensor_tensor(y, v3(d_z[j]), row(0), ALU.mult))
                ch.step(V.tensor_tensor(y, y, row(C), ALU.add))
                V.scalar_tensor_tensor(y, y, 0.0, v3(d_x[j]), ALU.max, ALU.add).then_inc(dsem["norm", "used"], 1)
                dve.wait_ge(dsem["norm", "used"], cnt(i, j) + 1)
                centre("norm", d_y, d_s, ch, j, None)
            pipeline(dve, TI, [(0, norm_res), (1, reduce("norm", d_sq, d_s)), (2, ln_out("norm", 1))], "dve", steps=R * 5)
            barrier(dve, "dve")


def kernel(**inp):
    import numpy as np
    import concourse.bacc as bacc
    from concourse.bass_utils import run_bass_kernel_spmd as run

    nc = bacc.Bacc("TRN2", target_bir_lowering=False, num_devices=1, dynamic_dma_scratch_size=8192)
    a = {k: np.asarray(v) for k, v in inp.items()}
    f = np.float32

    def padded(v, n, fill, front=()):
        out = np.full((len(front) + n,) + v.shape[1:], fill, v.dtype)
        if front:
            out[:len(front)] = front
        out[len(front):len(front) + len(v)] = v
        return out

    arrays = {
        "x": padded(a["x"], NP, 0),
        "src": padded(a["src"], EP, N),
        "dst": padded(a["dst"], EP + 1, N, front=(-1,)),
        "edge_t": np.ascontiguousarray(padded(a["edge_attr_32"], EP, 0).T),
        "gin_w1": a["L0_gnn_W1"], "gin_b1": a["L0_gnn_b1"], "gin_w2": a["L0_gnn_W2"], "gin_b2": a["L0_gnn_b2"],
        "cheb_w": np.concatenate([w.T for n in (2, 3, 4) for w in a[f"L3_gnn_w{n}"]], axis=1),
        "cheb_b": np.stack([a[f"L3_gnn_b{n}"] for n in (2, 3, 4)], axis=1),
        "att_w": a["L3_gnn_attn_w"].reshape(3, C, 3).transpose(1, 0, 2).reshape(C, 9),
        "att_b": np.concatenate([a["L3_gnn_fus_b"], a["L3_gnn_attn_b"], a["L3_gnn_fus_b"], a["L3_gnn_fus_b"]]),
        "fus_w": a["L3_gnn_fus_w"].reshape(3, C, C).transpose(1, 0, 2).reshape(C, 3 * C),
        "bn_g": a["L3_gnn_bn_gamma"], "bn_b": a["L3_gnn_bn_beta"],
    }
    arrays["dst"][-1] = N + 1
    for n in range(2):
        for part, name in (("msg", "_msg"), ("edge", "_edge"), ("root", "_root")):
            arrays[f"conv{n}_{part}"] = a[f"L2_gnn_W{n + 1}{name}"]
        arrays[f"conv{n}_b"] = a[f"L2_gnn_b{n + 1}"]
    arrays = {k: np.ascontiguousarray(v) for k, v in arrays.items()}
    t = {k: nc.dram_tensor("in_" + k, v.shape, mybir.dt.from_np(v.dtype), kind="ExternalInput").ap() for k, v in arrays.items()}
    t["out"] = nc.dram_tensor("out", (NP, C), F32, kind="ExternalOutput").ap()
    build(nc, t)
    r = run(nc, [{"in_" + k: v for k, v in arrays.items()}], core_ids=[0])
    return r.results[0]["out"][:N]
```

```python
import concourse.bass as bass
from concourse import mybir
from contextlib import ExitStack

F32 = mybir.dt.float32
F16 = mybir.dt.float16
BF16 = mybir.dt.bfloat16
I32 = mybir.dt.int32
U8 = mybir.dt.uint8
ALU = mybir.AluOpType
ACT = mybir.ActivationFunctionType
AX = mybir.AxisListType

N, E, C = 50000, 25000, 96
P = 128
Q = 4
GRP = P * Q
GROUPS = -(-E // GRP)
TILES = -(-N // GRP)
EP, NP = GROUPS * GRP, TILES * GRP
R = 7
GI, TI = GROUPS // R, TILES // R
assert GI * R == GROUPS and TI * R == TILES
QC = Q * C
FW = 3 * C + 3
TW = 100
HOPS = 16
ALPHA = 0.1
KEEP = 1.0 - ALPHA
EPS = 1e-5
BIG = 3.0e38
FAR = 1 << 17
IDX = GROUPS * Q


def build(nc, t):
    ctx = ExitStack()
    with ctx:
        sb = lambda n, s, d=F32: ctx.enter_context(nc.sbuf_tensor(n, s, d))
        sem = lambda n: ctx.enter_context(nc.semaphore(n))
        dram = lambda n, s: nc.dram_tensor(n, s, F32, kind="Internal").ap()

        aug = dram("aug", (NP, TW))
        hop_tab = dram("hop_tab", (NP + 2 * EP, C))
        x2_tab = dram("x2_tab", (NP + EP, C))
        c1_tab = dram("c1_tab", (NP + EP, C))
        x3_tab = dram("x3_tab", (NP, C))
        agg_tab = dram("agg_tab", (NP, C))
        q_tab = [dram("q1_tab", (EP + GRP, C)), dram("q2_tab", (EP + GRP, C))]
        p_slot = dram("p_slot", (EP, 2 * C))
        f_tab = dram("f_tab", (NP, FW))
        h_tab = dram("h_tab", (NP, C))

        ident = sb("ident", [P, P])
        keep = sb("keep", [P, EP], U8)
        src_i = sb("src_i", [P, IDX], I32)
        dst_i = sb("dst_i", [P, IDX], I32)
        put_i = sb("put_i", [P, IDX], I32)
        hop_i = [sb("hopa_i", [P, IDX], I32), sb("hopb_i", [P, IDX], I32)]
        q_i = sb("q_i", [P, IDX], I32)
        sd_in = sb("sd_in", [P, IDX])
        w_hop = sb("w_hop", [P, IDX])
        w_out = sb("w_out", [P, IDX])
        w_src = sb("w_src", [P, IDX])
        ln_s = sb("ln_s", [P, R, 4 * Q])
        w_root = [sb("w_root0", [P, C]), sb("w_root1", [P, C])]
        get_st = sb("get_st", [P, R, Q], I32)
        put_st = sb("put_st", [P, R, Q], I32)
        G = sb("G", [P, R, Q * TW])
        sc = sb("sc", [P, 3, GRP])
        eps_col = sb("eps_col", [P, 1])
        eps2_col = sb("eps2_col", [P, 1])
        zero_row = sb("zero_row", [P, FW])
        tmp = sb("tmp", [P, 3, QC])
        out_r = sb("out_r", [P, R, QC])
        out_rows = [out_r[:, j, :] for j in range(R)]
        hop_s = [ln_s[:, j, :] for j in range(R)]
        free = out_r[:, :, :].rearrange("p j n -> p (j n)")
        n_x, n_t, n_c, n_t2, n_y, n_sq = (free[:, a:a + w] for a, w in
                                         ((0, QC), (QC, GRP), (QC + GRP, QC), (2 * QC + GRP, GRP), (2 * (QC + GRP), QC), (3 * QC + 2 * GRP, QC)))
        assert 4 * QC + 2 * GRP <= R * QC
        big = sb("big", [P, 2, IDX * C])
        state, g0 = big[:, 0, :], big[:, 1, :]

        def carve(at, cols, parts=P):
            flat = big[:, :, :].rearrange("p a n -> p (a n)")
            assert at + cols <= 2 * IDX * C
            return flat[0:parts, at:at + cols]

        ps = ctx.enter_context(nc.psum_tensor("ps", [P, 8, 512], F32))
        bank = [ps[:, b, :] for b in range(8)]
        pin, pout, pmm = bank[0:3], bank[3:6], bank[6:8]

        setup_ld = sem("setup_ld")
        bar = sem("bar")
        chain_s = {e: sem("chain_" + e) for e in ("dve", "act", "pool")}
        got = [sem(f"got{j}") for j in range(R)]
        put = [sem(f"put{j}") for j in range(R)]
        staged = sem("staged")
        put_staged = sem("put_staged")
        taken = sem("taken")
        moved = sem("moved")
        mixed = sem("mixed")
        scanned = sem("scanned")
        tout = sem("tout")
        done = sem("done")
        freed = sem("freed")
        keeps = sem("keeps")
        pool_turn = sem("pool_turn")
        wr = [sem(f"wr{j}") for j in range(R)]
        ld = [sem(f"ld{j}") for j in range(R)]
        st = [sem(f"st{j}") for j in range(R)]

        def ge(eng, s, v):
            if isinstance(v, int) and v <= 0:
                return
            eng.wait_ge(s, v)

        class Chain:
            def __init__(self, eng, name, at=0):
                self.eng, self.s, self.at, self.n = eng, chain_s[name], at, 0

            def step(self, ins):
                ins.then_inc(self.s, 1)
                self.n += 1
                self.eng.wait_ge(self.s, self.at + self.n)

        chain_at = {"dve": 0, "act": 0, "pool": 0}

        def straight(eng, name):
            return Chain(eng, name, chain_at[name])

        def end_straight(ch, name):
            chain_at[name] += ch.n

        def loop(eng, n, body, name=None, steps=0, first=True):
            at = chain_at[name] if name else 0

            def once(i):
                ch = Chain(eng, name, at + steps * i) if name else None
                body(i, ch)
                assert ch is None or ch.n == steps, (ch.n, steps)
            lo = 0
            if first:
                once(0)
                lo = 1
            if n > lo:
                with eng.Fori(lo, n) as i:
                    once(i)
            if name:
                chain_at[name] += steps * n

        barriers = {"n": {}}

        def barrier(eng, name, passing=False):
            k = barriers["n"].get(name, 0) + 1
            barriers["n"][name] = k
            eng.drain().then_inc(bar, 1)
            if not passing:
                eng.wait_ge(bar, 5 * k)


        S3, GAP3 = [0, 1, 0, 1, 0, 1, 2], [3, 3, 2, 2, 2, 2, 6]
        S2, GAP2 = [0, 1, 0, 1, 0, 1, 0], [1, 3, 2, 2, 2, 2, 2]

        def rows(tab, i, j, base=0, w=None):
            part = tab[bass.ds(i * (R * GRP) + (j * GRP + base), GRP), :]
            if w is not None:
                part = part[:, w[0]:w[1]]
            return part.rearrange("(p q) c -> p q c", p=P)

        def at(i, j, w, n=None, off=0):
            return bass.ds(i * (R * w) + (j * w + off), n or w)

        def v3(ap, w=C):
            return ap.rearrange("p (q c) -> p q c", c=w)

        def spread(ap):
            return ap.unsqueeze(2).to_broadcast([P, Q, C])

        SUM0, DSTS, HOP1, HOP2, HOPL, MAX1, MAX2, CHEB1, CHEB2, CHEB3 = 0, 1, 2, 3, 17, 18, 19, 20, 21, 22
        ROUNDS = (HOPL - HOP2) // 2

        def scans(k):
            return k if isinstance(k, int) and k <= DSTS else k - 1

        SCATTERS = (SUM0, MAX2, CHEB3)

        def lagged(i, j, lag):
            if j >= lag:
                return i, j - lag
            return (None, None) if isinstance(i, int) and i == 0 else (i - 1, j - lag + R)

        def pipeline(eng, n, stages, name=None, steps=0, start=None, peel=1):
            top = max(lag for lag, _ in stages)
            base = (chain_at[name] if start is None else start) if name else 0
            per = steps

            def body(i, upto=R, tail=False):
                full = not (isinstance(i, int) and i == 0) and not tail
                ch = None
                if name:
                    start = base if isinstance(i, int) and i == 0 else base + (firstn["n"] + (i - 1) * per if not tail else firstn["n"] + (n - 1) * per)
                    ch = Chain(eng, name, start)
                for j in range(upto):
                    for lag, f in stages:
                        if tail and j >= lag:
                            continue
                        a, b = lagged(i, j, lag)
                        if a is not None:
                            f(a, b, ch)
                return ch
            firstn = {"n": 0}
            ch = body(0)
            if ch:
                firstn["n"] = ch.n
            assert peel == 1 or not name
            for i in range(1, peel):
                body(i)
            if n > peel:
                with eng.Fori(peel, n) as i:
                    ch = body(i)
                    assert ch is None or ch.n == per, (name, ch.n, per)
            tail = body(n, upto=top, tail=True)
            if name and start is None:
                chain_at[name] = base + firstn["n"] + (n - 1) * per + tail.n

        CREDIT = 16

        def bases(table, total=0):
            out = {}
            for phase, per, n in table:
                out[phase] = total
                total += 16 * per * n
            return out

        LD = bases([("keep", 1, GI), ("gin", 2, TI), ("max1", 2, GI), ("max2", 3, GI), ("cheb3", 1, GI), ("attend", 2, TI), ("norm", 2, TI)])
        ST = bases([("gin", 3, TI), ("attend", 1, TI), ("norm", 1, TI)], CREDIT)
        WR = bases([("hops", 1, GI * HOPS), ("x2_slot", 1, GI), ("c1_slot", 1, GI), ("cheb1", 2, GI), ("cheb2", 2, GI)])
        PUT = bases([(k, Q, GI) for k in SCATTERS])

        def ring(start, cols, n=R, parts=P):
            return [carve(start + s * cols, cols, parts) for s in range(n)], start + n * cols

        edge_f, o = ring(0, 4 * IDX, 1)
        lo_hi = edge_f[0].rearrange("p (k n) -> p k n", k=4)
        onehot, o = ring(o, 2 * (GRP + P) // 2, Q)
        keep_ld, o = ring(o, GRP + 1)
        iota_lo, o = ring(o, GRP // 2, 1)
        iota_hi, o = ring(o, P // 2, 1)
        zeros, o = ring(o, R * QC, 1)
        node_sc_, o = ring(o, 3 * TILES * Q, 1)
        node_sc = node_sc_[0].rearrange("p (k n) -> p k n", k=3)
        deg, o = ring(o, GRP, 10)
        tri, o = ring(o, P, 1)
        w_gin1, o = ring(o, C, 1)
        w_gin2, o = ring(o, C, 1)
        b_gin1, o = ring(o, 1, 1)
        gin_x, o = ring(o, QC)
        gin_z, o = ring(o, QC)
        gin_r, o = ring(o, GRP, 3)
        gin_h, o = ring(o, GRP, 3)
        gin_y, o = ring(o, QC)
        gin_s, o = ring(o, 7 * Q)
        gin_sq, o = ring(o, QC, 3)
        gin_o, o = ring(o, QC)
        gin_a, o = ring(o, Q * TW)
        gin_u, o = ring(o, QC)
        o = 0
        neg, o = ring(o, EP // 2, 1)
        neg = neg[0].bitcast(BF16)
        w_mix, o = ring(o, C, 2)
        mix_r, o = ring(o, GRP, 3)
        late0 = o
        d_x, o = ring(o, QC)
        d_z, o = ring(o, QC)
        d_w, o = ring(o, QC)
        d_t, o = ring(o, GRP, 3)
        d_y, o = ring(o, QC)
        d_s, o = ring(o, 4 * Q)
        d_sq, o = ring(o, QC, 3)
        d_o, o = ring(o, QC)
        o = late0
        w_feat, o = ring(o, FW, 4)
        bn, o = ring(o, 16, 1)
        late1 = o
        cheb_a, o = ring(o, QC)
        cheb_b, o = ring(o, QC)
        cheb_p, o = ring(o, 3 * QC, 3)
        cheb_t, o = ring(o, GRP, 6)
        cheb_f, o = ring(o, Q * FW)
        o = late1
        a_x, o = ring(o, QC)
        a_f, o = ring(o, Q * FW)
        a_t, o = ring(o, GRP, 3)
        a_h, o = ring(o, QC)
        a_s, o = ring(o, 8 * Q)
        stats, o = ring(o, TILES * 6, 1)
        assert o < late1 + 20000
        bn_wide, o = ring(late1 + 20000, P, 2)
        bn_row, o = ring(o, 2 * C, 1)
        o = late1
        wt, o = ring(o, 9 * C, 1)
        wh, o = ring(o, 9 * (C + 1), 1)
        wb, o = ring(o, 3, 1)
        att, o = ring(o, 9, 1)
        fus, o = ring(o, 3 * C, 1)
        att_b, o = ring(o, FW, 1)
        FEATS = [((0, 1), 195), ((0, 1, 2), 99), ((0, 1, 2, 3), 0)]
        LOGIT, WIDE, filt_at = C, [291, 291, 195, 99], [0, 2, 5]

        dsem = {(ph, n): sem(f"{ph}_{n}") for ph, ns in {
            "gin": "summed turned copied mixed1 relued mixed2 used centred squared rooted final widened",
            "hopl": "centred squared rooted",
            "own": "summed turned copied mixed leaked centred squared reduced rooted final",
            "conv": "turned copied centred squared reduced rooted",
            "attend": "turned copied mixed2 topped raised summed scaled weighed shared joined used turned2 final",
            "norm": "shifted used centred squared rooted final"}.items() for n in ns.split()}
        one = {n: sem(n) for n in "idents hot histed cleared puts zeroed step_pe step_dve step_act prep_ld ones_set".split()}
        table_written = sem("table_written")
        fturned = sem("fturned")
        fcopied = sem("fcopied")
        fmixed = sem("fmixed")
        fread = sem("fread")
        thirds = sem("thirds")
        own_ld, own_c, own_x = sem("own_ld"), sem("own_c"), sem("own_x")
        negated = sem("negated")
        prescaled = sem("prescaled")
        outdone = sem("outdone")
        put_ready = sem("put_ready")
        KU = {SUM0: 0, MAX2: 1, CHEB3: 2}
        OU = {HOPL: 0, MAX1: 1, MAX2: 2}

        FBANK, FGAP = [4, 5, 4], [1, 3, 2]
        FCREDIT = 4 * 2
        nload = {"max1": 2, "max2": 3}

        def own_tile(u, i):
            return u * GI + i
        assert 2 * ROUNDS * GI == TILES

        def cnt(i, j):
            return i * R + j

        block = ctx.enter_context(nc.Block())

        @block.sync
        def _(sp):
            for s_ in st:
                sp.sem_inc(s_, CREDIT)
            sp.dma_start(src_i[:, :], t["src"].rearrange("(t p q) -> p t q", p=P, q=Q)).then_inc(setup_ld, 16)
            sp.dma_start(dst_i[:, :], t["dst"][1:EP + 1].rearrange("(t p q) -> p t q", p=P, q=Q)).then_inc(setup_ld, 16)
            sp.dma_start(put_i[:, :], t["dst"][2:EP + 2].rearrange("(t p q) -> p t q", p=P, q=Q)).then_inc(setup_ld, 16)
            sp.dma_start(w_gin1[0][0:C, :], t["gin_w1"]).then_inc(setup_ld, 16)
            sp.dma_start(w_gin2[0][0:C, :], t["gin_w2"]).then_inc(setup_ld, 16)
            sp.dma_start(w_gin2[0][C:C + 1, :], t["gin_b2"].rearrange("(o c) -> o c", o=1)).then_inc(setup_ld, 16)
            sp.dma_start(b_gin1[0][0:C, :], t["gin_b1"].rearrange("(c o) -> c o", o=1)).then_inc(setup_ld, 16)
            for n in range(2):
                sp.dma_start(w_root[n][0:C, :], t[f"conv{n}_root"]).then_inc(setup_ld, 16)
                sp.dma_start(w_root[n][C:C + 1, :], t[f"conv{n}_b"].rearrange("(o c) -> o c", o=1)).then_inc(setup_ld, 16)

            def load_dst(i, j, ch):
                ge(sp, keeps, cnt(i, j) - R + 1)
                sp.dma_start(keep_ld[j].bitcast(I32)[0:C, :], t["dst"][bass.ds(i * (R * GRP) + j * GRP, GRP + 1)].partition_broadcast(C)).then_inc(ld[j], 16)
            pipeline(sp, GI, [(0, load_dst)])
            barrier(sp, "sp")
            barrier(sp, "sp")
            for q in q_tab:
                sp.dma_start(q[EP:EP + GRP, :].rearrange("(p q) c -> p q c", p=P), v3(zeros[0][:, 0:QC])).then_inc(one["zeroed"], 16)
            sp.wait_ge(one["zeroed"], 16 * (TI + 2))

            def dense(ph, loads, stores, per=1):
                def load(i, j, ch):
                    ge(sp, dsem[ph, "used"], per * (cnt(i, j) - R + 1))
                    for dst, src, w in loads:
                        sp.dma_start(v3(dst[j], w), rows(src, i, j)).then_inc(ld[j], 16)

                def store(i, j, ch):
                    ge(sp, dsem[ph, "used" if ph == "attend" else "final"], cnt(i, j) + 1)
                    if ph == "gin":
                        ge(sp, dsem[ph, "widened"], cnt(i, j) + 1)
                    for src, dst, w in stores:
                        sp.dma_start(rows(dst, i, j), v3(src[j], w)).then_inc(st[j], 16)
                pipeline(sp, TI, [(0, load), (R, store)])
                for j in range(R):
                    sp.wait_ge(st[j], ST[ph] + 16 * len(stores) * TI)
                barrier(sp, "sp")

            dense("gin", [(gin_x, t["x"], C), (gin_z, agg_tab, C)], [(gin_o, hop_tab, C), (gin_a, aug, TW), (gin_u, x2_tab, C)])

            def node_rows(tab, u, i):
                return tab[bass.ds(own_tile(u, i) * GRP, GRP), :].rearrange("(p q) c -> p q c", p=P)

            def own_io(u, i, j):
                T = own_tile(u, i)
                if j == 0:
                    sp.wait_ge(dsem["own", "summed"], T + 1)
                    sp.dma_start(v3(n_x), node_rows(x2_tab, u, i)).then_inc(own_ld, 16)
                if j == 2:
                    sp.dma_start(node_rows(f_tab, u, i), zero_row[:, :].unsqueeze(1).to_broadcast([P, Q, FW])).then_inc(one["zeroed"], 16)
                if j == 4:
                    sp.wait_ge(dsem["own", "leaked"], T + 1)
                    sp.dma_start(node_rows(c1_tab, u, i), v3(n_c)).then_inc(own_c, 16)
                if j == R - 1:
                    sp.wait_ge(dsem["own", "final"], T + 1)
                    sp.dma_start(node_rows(x3_tab, u, i), v3(n_y)).then_inc(own_x, 16)

            def hop_store(k, h, parity, u=None):
                def store(i, j):
                    sp.wait_ge(done, h * GROUPS + cnt(i, j) + 1)
                    for n in ((0, 1) if k == HOP1 else (parity,)):
                        sp.dma_start(rows(hop_tab, i, j, NP + n * EP), v3(state[:, at(i, j, QC)])).then_inc(wr[j], 16)
                with sp.Fori(0, GI) as i:
                    for j in range(R):
                        if u is not None and j == 0:
                            own_io(u, i, j)
                        store(i, j)
                        if u is not None and j:
                            own_io(u, i, j)
                for j in range(R):
                    sp.wait_ge(wr[j], h * (16 * GI) + 32 * GI)
                sp.sem_inc(table_written, 1)
            hop_store(HOP1, 0, 0)
            barrier(sp, "sp")
            with sp.Fori(0, ROUNDS) as r:
                hop_store(None, r * 2 + 1, 1, r * 2)
                hop_store(None, r * 2 + 2, 0, r * 2 + 1)
            sp.wait_ge(own_c, 16 * (TILES + 1))
            sp.wait_ge(own_x, 16 * (TILES + 1))
            sp.wait_ge(one["zeroed"], 16 * (TI + 2 + TILES))

            def slot_store(k, tab):
                def f(i, j, ch=None):
                    sp.wait_ge(outdone, OU[k] * GROUPS + cnt(i, j) + 1)
                    sp.dma_start(rows(tab, i, j, NP), v3(out_rows[j])).then_inc(wr[j], 16)
                return f
            f = slot_store(HOPL, x2_tab)
            with sp.Fori(0, GI) as i:
                for j in range(R):
                    f(i, j)
            for j in range(R):
                sp.wait_ge(wr[j], WR["x2_slot"] + 16 * GI)
            barrier(sp, "sp")

            for n in range(2):
                sp.dma_start(w_mix[n][0:C, :], t[f"conv{n}_msg"]).then_inc(one["prep_ld"], 16)
                sp.dma_start(w_mix[n][C:P, :], t[f"conv{n}_edge"]).then_inc(one["prep_ld"], 16)

            for n, (k, ph) in enumerate(((MAX1, "max1"), (MAX2, "max2"))):
                def load_edges(i, j, ch):
                    ge(sp, mixed, n * GROUPS + cnt(i, j) - GAP3[j] + 1)
                    sp.dma_start(mix_r[S3[j]][C:P, :], t["edge_t"][:, bass.ds(i * (R * GRP) + j * GRP, GRP)]).then_inc(ld[j], 16)
                    ge(sp, outdone, OU[k] * GROUPS + cnt(i, j) - R + 1)
                    sp.dma_start(v3(d_x[j]), rows(c1_tab if n else x2_tab, i, j, NP)).then_inc(ld[j], 16)
                    if n:
                        sp.dma_start(v3(d_w[j]), rows(x2_tab, i, j, NP)).then_inc(ld[j], 16)
                pipeline(sp, GI, [(0, load_edges)] + ([] if n else [(4, slot_store(MAX1, c1_tab))]))
                if n == 0:
                    for j in range(R):
                        sp.wait_ge(wr[j], WR["c1_slot"] + 16 * GI)
                barrier(sp, "sp")

            for dst, src in ((wt[0][0:C, :], t["cheb_w"]), (wb[0][0:C, :], t["cheb_b"]), (att[0][0:C, :], t["att_w"]),
                             (att_b[0][C:C + 1, :], t["att_b"].rearrange("(o c) -> o c", o=1)),
                             (fus[0][0:C, :], t["fus_w"]),
                             (bn[0][0:C, 4:5], t["bn_g"].rearrange("(c o) -> c o", o=1)),
                             (bn[0][0:C, 5:6], t["bn_b"].rearrange("(c o) -> c o", o=1))):
                sp.dma_start(dst, src).then_inc(one["prep_ld"], 16)
            barrier(sp, "sp")
            for n, ph in enumerate(("cheb1", "cheb2")):
                def store_cheb(i, j, ch):
                    sp.wait_ge(done, (HOPS - 1 + n) * GROUPS + cnt(i, j) + 1)
                    sp.dma_start(rows(p_slot, i, j, w=(n * C, n * C + C)), v3(cheb_a[j])).then_inc(wr[j], 16)
                    sp.dma_start(rows(q_tab[n], i, j), v3(cheb_b[j])).then_inc(wr[j], 16)
                with sp.Fori(0, GI) as i:
                    for j in range(R):
                        store_cheb(i, j, None)
                for j in range(R):
                    sp.wait_ge(wr[j], WR[ph] + 32 * GI)
                barrier(sp, "sp")

            def load_p(i, j, ch):
                ge(sp, fturned, 3 * (cnt(i, j) - GAP3[j] + 1))
                sp.dma_start(v3(cheb_p[S3[j]], 3 * C)[:, :, 0:2 * C], rows(p_slot, i, j)).then_inc(ld[j], 16)
            pipeline(sp, GI, [(0, load_p)])
            barrier(sp, "sp")

            dense("attend", [(a_x, x3_tab, C), (a_f, f_tab, FW)], [(a_h, h_tab, C)])
            barrier(sp, "sp")
            dense("norm", [(d_x, x3_tab, C), (d_z, h_tab, C)], [(d_o, t["out"], C)])

        @block.gpsimd
        def _(pl):
            ch = straight(pl, "pool")
            ch.step(nc.gpsimd.memset(ident[:, :], 0.0))
            ch.step(nc.gpsimd.affine_select(out=ident[:, :], in_=ident[:, :], compare_op=ALU.not_equal, fill=1.0,
                                            base=0, pattern=[[-1, P]], channel_multiplier=1))
            ch.step(nc.gpsimd.memset(tri[0], 1.0))
            ch.step(nc.gpsimd.affine_select(out=tri[0], in_=tri[0], compare_op=ALU.is_gt, fill=0.0,
                                            base=0, pattern=[[1, P]], channel_multiplier=-1))
            ch.step(nc.gpsimd.iota(iota_lo[0].bitcast(F16), [[1, GRP]], base=0, channel_multiplier=0, allow_small_or_imprecise_dtypes=True))
            ch.step(nc.gpsimd.iota(iota_hi[0].bitcast(F16), [[1, P]], base=0, channel_multiplier=0, allow_small_or_imprecise_dtypes=True))
            ch.step(nc.gpsimd.iota(deg[9][0:TILES, :], [[1, GRP]], base=0, channel_multiplier=GRP, allow_small_or_imprecise_dtypes=True))
            pl.sem_inc(one["idents"], 1)
            end_straight(ch, "pool")

            def gather(k, table, w):
                def f(i, j, ch=None):
                    pl.wait_ge(staged, k * GROUPS + cnt(i, j) + 1)
                    pl.sem_inc(pool_turn, 1)
                    for q in range(Q):
                        pl.indirect_dma_start(G[:, j, q * w:q * w + w], None, table,
                                              bass.IndirectOffsetOnAxis(ap=get_st[:, j, q:q + 1], axis=0)).then_inc(got[j], 16)
                return f

            def scatter(k, table, w, src):
                def f(i, j, ch=None):
                    if isinstance(k, int) and k == SUM0:
                        pl.wait_ge(one["zeroed"], 16 * TI)
                    pl.wait_ge(put_ready, KU[k] * GROUPS + cnt(i, j) + 1)
                    pl.sem_inc(pool_turn, 1)
                    if k in OU:
                        pl.wait_ge(outdone, OU[k] * GROUPS + cnt(i, j) + 1)
                    elif k == CHEB3:
                        pl.wait_ge(fread, 4 * cnt(i, j) + 4)
                    else:
                        pl.wait_ge(freed, scans(k) * GROUPS + cnt(i, j) + 1)
                    pl.sem_inc(pool_turn, 1)
                    for q in range(Q):
                        pl.indirect_dma_start(table, bass.IndirectOffsetOnAxis(ap=put_st[:, j, q:q + 1], axis=0),
                                              src[j][:, q * w:q * w + w], None, bounds_check=NP - 1, oob_is_err=False).then_inc(put[j], 16)
                return f

            def scatter_pass(k, table, w, to, tw, src):
                pipeline(pl, GI, [(0, gather(k, table, w)), (R, scatter(k, to, tw, src))])
                for j in range(R):
                    pl.wait_ge(put[j], PUT[k] + 64 * GI)
                barrier(pl, "pool")

            def gather_pass(k, table, w):
                f = gather(k, table, w)
                with pl.Fori(0, GI) as i:
                    for j in range(R):
                        f(i, j)

            scatter_pass(SUM0, t["x"], C, agg_tab, C, out_rows)
            barrier(pl, "pool")

            def gin_sum(i, j, ch):
                pl.wait_ge(ld[j], LD["gin"] + 32 * (i + 1))
                nc.gpsimd.tensor_tensor(gin_z[j], gin_z[j], gin_x[j], ALU.add).then_inc(dsem["gin", "summed"], 1)

            def gin_wide(i, j, ch):
                pl.wait_ge(dsem["gin", "final"], cnt(i, j) + 1)
                ge(pl, st[j], ST["gin"] + 48 * i)
                row = v3(gin_a[j], TW)
                sc_ = node_sc[:, :, at(i, j, Q)]
                nc.gpsimd.tensor_copy(row[:, :, C:C + 3], sc_.rearrange("p k q -> p q k"))
                nc.gpsimd.tensor_tensor(row[:, :, 0:C], v3(gin_o[j]), spread(sc_[:, 1, :]), ALU.mult).then_inc(dsem["gin", "widened"], 1)
            pipeline(pl, TI, [(0, gin_sum), (5, gin_wide)])
            barrier(pl, "pool")
            gather_pass(DSTS, aug, TW)
            gather_pass(HOP1, aug, TW)
            barrier(pl, "pool")
            with pl.Fori(0, ROUNDS) as r:
                gather_pass(r * 2 + HOP2, hop_tab, C)
                gather_pass(r * 2 + (HOP2 + 1), hop_tab, C)
            gather_pass(HOPL, hop_tab, C)
            barrier(pl, "pool")
            gather_pass(MAX1, x2_tab, C)
            barrier(pl, "pool")
            scatter_pass(MAX2, c1_tab, C, x3_tab, C, out_rows)
            barrier(pl, "pool", passing=True)
            gather_pass(CHEB1, x3_tab, C)
            barrier(pl, "pool")
            gather_pass(CHEB2, q_tab[0], C)
            barrier(pl, "pool")
            scatter_pass(CHEB3, q_tab[1], C, f_tab, FW, cheb_f)

            def a_first(i, j, ch):
                f_, col = v3(a_f[j], FW), FEATS[0][1]
                e = a_s[j][:, Q:4 * Q].rearrange("p (q k) -> p q k", k=3)[:, :, 0:1].to_broadcast([P, Q, C])
                pl.wait_ge(dsem["attend", "scaled"], cnt(i, j) + 1)
                nc.gpsimd.tensor_tensor(f_[:, :, col:col + C], f_[:, :, col:col + C], e, ALU.mult).then_inc(dsem["attend", "weighed"], 1)

            def a_join(i, j, ch):
                f_, c0, c1 = v3(a_f[j], FW), FEATS[0][1], FEATS[1][1]
                pl.wait_ge(dsem["attend", "weighed"], cnt(i, j) + 1)
                pl.wait_ge(dsem["attend", "shared"], cnt(i, j) + 1)
                nc.gpsimd.tensor_tensor(f_[:, :, c0:c0 + C], f_[:, :, c0:c0 + C], f_[:, :, c1:c1 + C], ALU.add).then_inc(dsem["attend", "joined"], 1)
            pipeline(pl, TI, [(0, a_first), (0, a_join)])
            barrier(pl, "pool")
            barrier(pl, "pool")

            def norm_shift(i, j, ch):
                pl.wait_ge(ld[j], LD["norm"] + 32 * (i + 1))
                z = v3(d_z[j])
                row = lambda a: bn_row[0][:, a:a + C].unsqueeze(1).to_broadcast([P, Q, C])
                ch.step(nc.gpsimd.tensor_tensor(z, z, row(0), ALU.mult))
                nc.gpsimd.tensor_tensor(z, z, row(C), ALU.add).then_inc(dsem["norm", "shifted"], 1)
            pipeline(pl, TI, [(0, norm_shift)], "pool", steps=R)
            barrier(pl, "pool")

        @block.tensor
        def _(pe):
            def turn(k, extra=None, before=None, w=C, ring_=(pin, S3, GAP3)):
                banks, S, GAP = ring_

                def f(i, j, ch=None):
                    g = cnt(i, j)
                    if before is not None:
                        pe.wait_ge(before, g + 1)
                    ge(pe, got[j], 64 * (k * GI + i + 1))
                    if extra == "max":
                        ge(pe, moved, (k - MAX1 + 1) * GROUPS + g - GAP[j] + 1)
                    else:
                        ge(pe, scanned, scans(k) * GROUPS + g - GAP[j] + 1)
                    for q in range(Q):
                        last = nc.tensor.transpose(banks[S[j]][0:C, q::Q], G[:, j, q * w:q * w + C], ident[:, :])
                    last.then_inc(taken, 1)
                return f

            def turn_back(k, ring_=(pout, S3, GAP3)):
                banks, S, GAP = ring_

                def f(i, j, ch=None):
                    g = scans(k) * GROUPS + cnt(i, j)
                    pe.wait_ge(scanned, g + 1)
                    ge(pe, freed, g - GAP[j] + 1)
                    for q in range(Q):
                        last = nc.tensor.transpose(banks[S[j]][:, q * C:q * C + C], sc[0:C, S3[j], q::Q], ident[0:C, 0:C])
                    last.then_inc(tout, 1)
                return f

            def hist(i, j, ch):
                for q in range(Q):
                    pe.wait_ge(one["hot"], 4 * cnt(i, j) + q + 1)
                    row = onehot[q].bitcast(F16).rearrange("p (k n) -> p k n", k=2)
                    for k in range(2):
                        first = isinstance(i, int) and i == 0 and j == 0 and q == 0
                        last = nc.tensor.matmul(pmm[k][0:TILES, :], row[:, k, GRP:GRP + TILES], row[:, k, 0:GRP],
                                                start=first, stop=False, skip_group_check=True)
                    last.then_inc(one["histed"], 1)

            pe.wait_ge(one["idents"], 1)
            pe.wait_ge(one["cleared"], 1)
            pipeline(pe, GI, [(0, turn(SUM0)), (0, hist), (0, turn_back(SUM0))])
            for k in range(2):
                nc.tensor.matmul(pmm[k][0:TILES, :], zeros[0].bitcast(F16)[:, 0:TILES], zeros[0].bitcast(F16)[:, 0:GRP],
                                 start=False, stop=True, skip_group_check=True)
            barrier(pe, "pe")
            pe.wait_ge(one["step_dve"], 1)
            nc.tensor.matmul(bank[0][0:TILES, 0:1], tri[0][0:TILES, 0:TILES], deg[2][0:TILES, GRP - 1:GRP],
                             start=True, stop=True).then_inc(one["step_pe"], 1)
            pe.wait_ge(one["step_dve"], 3)
            for n, d in enumerate((6, 7, 8)):
                for q in range(Q):
                    last = nc.tensor.transpose(bank[3 + n][:, q * TILES:(q + 1) * TILES], deg[d][0:TILES, q::Q], ident[0:TILES, 0:TILES])
            last.then_inc(one["step_pe"], 1)
            barrier(pe, "pe")

            def dturn(ph, src, ready, w=C, k=0):
                def f(i, j, ch):
                    if ready is None:
                        pe.wait_ge(ld[j], LD[ph] + 16 * nload[ph] * (i + 1))
                    else:
                        pe.wait_ge(dsem[ph, ready], cnt(i, j) + 1)
                    ge(pe, dsem[ph, "copied"], cnt(i, j) - GAP3[j] + 1)
                    for q in range(Q):
                        last = nc.tensor.transpose(pin[S3[j]][0:C, q * P:(q + 1) * P], src[j][:, q * C:q * C + C], ident[:, :])
                    last.then_inc(dsem[ph, "turned"], 1)
                return f

            def product(ph, lhs, weights, ready):
                def f(i, j, ch):
                    pe.wait_ge(dsem[ph, ready], cnt(i, j) + 1)
                    ge(pe, dsem[ph, "used"], cnt(i, j) - GAP2[j] + 1)
                    for q in range(Q):
                        last = nc.tensor.matmul(pmm[S2[j]][:, q * C:q * C + C], lhs[S3[j]][0:C + 1, q * P:(q + 1) * P], weights[0:C + 1, :],
                                                start=True, stop=True)
                    last.then_inc(dsem[ph, "mixed2"], 1)
                return f

            def gin_first(i, j, ch):
                pe.wait_ge(dsem["gin", "copied"], cnt(i, j) + 1)
                ge(pe, dsem["gin", "relued"], cnt(i, j) - GAP3[j] + 1)
                nc.tensor.matmul(pout[S3[j]][0:C, :], w_gin1[0][0:C, :], gin_r[S3[j]][0:C, :],
                                 start=True, stop=True).then_inc(dsem["gin", "mixed1"], 1)

            pe.wait_ge(setup_ld, 16 * 11)
            pipeline(pe, TI, [(0, dturn("gin", gin_z, "summed")), (1, gin_first), (2, product("gin", gin_h, w_gin2[0], "relued"))])
            barrier(pe, "pe")

            def own_pe(u, i, j):
                T = own_tile(u, i)
                if j == 1:
                    pe.wait_ge(own_ld, 16 * T + 16)
                    pe.wait_ge(dsem["own", "copied"], 2 * T + 2)
                    for q in range(Q):
                        last = nc.tensor.transpose(pmm[0][0:C, q * P:(q + 1) * P], n_x[:, q * C:q * C + C], ident[:, :])
                    last.then_inc(dsem["own", "turned"], 1)
                if j == 2:
                    pe.wait_ge(dsem["own", "copied"], 2 * T + 3)
                    pe.wait_ge(dsem["own", "summed"], T + 1)
                    for q in range(Q):
                        last = nc.tensor.matmul(pmm[1][:, q * C:q * C + C], n_t[0:C + 1, q * P:(q + 1) * P], w_root[0][0:C + 1, :],
                                                start=True, stop=True)
                    last.then_inc(dsem["own", "mixed"], 1)
                if j == 3:
                    pe.wait_ge(dsem["own", "leaked"], T + 1)
                    for q in range(Q):
                        last = nc.tensor.transpose(pmm[0][0:C, q * P:(q + 1) * P], n_c[:, q * C:q * C + C], ident[:, :])
                    last.then_inc(dsem["own", "turned"], 1)
                if j == 4:
                    pe.wait_ge(dsem["own", "copied"], 2 * T + 4)
                    for q in range(Q):
                        last = nc.tensor.matmul(pmm[1][:, q * C:q * C + C], n_t2[0:C + 1, q * P:(q + 1) * P], w_root[1][0:C + 1, :],
                                                start=True, stop=True)
                    last.then_inc(dsem["own", "mixed"], 1)

            def scan_pass(k, before=None, w=C, u=None):
                a, b = turn(k, before=before, w=w), turn_back(k)
                own = [(0, lambda i, j, ch: own_pe(u, i, j))] if u is not None else []
                pipeline(pe, GI, [(0, a), (1, b)] + own)
            scan_pass(HOP1, before=moved, w=TW)
            barrier(pe, "pe")
            pe.sem_inc(dsem["own", "mixed"], 2)
            with pe.Fori(0, ROUNDS) as r:
                scan_pass(r * 2 + HOP2, u=r * 2)
                scan_pass(r * 2 + (HOP2 + 1), u=r * 2 + 1)
            scan_pass(HOPL)
            barrier(pe, "pe")

            pe.wait_ge(one["prep_ld"], 16 * 4)
            pe.wait_ge(one["cleared"], 2)

            for n, (k, ph) in enumerate(((MAX1, "max1"), (MAX2, "max2"))):
                def mix(i, j, ch):
                    g = n * GROUPS + cnt(i, j)
                    pe.wait_ge(moved, GROUPS + g + 1)
                    pe.wait_ge(ld[j], LD[ph] + 16 * nload[ph] * (i + 1))
                    ge(pe, scanned, scans(k) * GROUPS + cnt(i, j) - GAP2[j] + 1)
                    nc.tensor.matmul(pmm[S2[j]][0:C, :], w_mix[n], mix_r[S3[j]][:, :], start=True, stop=True).then_inc(mixed, 1)

                def conv_turn(i, j, ch):
                    pe.wait_ge(ld[j], LD[ph] + 16 * nload[ph] * (i + 1))
                    ge(pe, dsem["conv", "copied"], n * GROUPS + cnt(i, j))
                    for q in range(Q):
                        last = nc.tensor.transpose(bank[2][0:C, q * P:(q + 1) * P], d_x[j][:, q * C:q * C + C], ident[:, :])
                    last.then_inc(dsem["conv", "turned"], 1)

                def conv_root(i, j, ch):
                    g = n * GROUPS + cnt(i, j)
                    pe.wait_ge(dsem["conv", "copied"], g + 1)
                    pe.wait_ge(scanned, scans(k) * GROUPS + cnt(i, j) + 1)
                    ge(pe, freed, scans(k) * GROUPS + cnt(i, j) - GAP3[j] + 1)
                    for q in range(Q):
                        o_ = pout[S3[j]][:, q * C:q * C + C]
                        nc.tensor.matmul(o_, d_t[S3[j]][0:C + 1, q * P:(q + 1) * P], w_root[n][0:C + 1, :], start=True, stop=False)
                        last = nc.tensor.matmul(o_, sc[0:C, S3[j], q::Q], ident[0:C, 0:C], start=False, stop=True)
                    last.then_inc(tout, 1)
                pipeline(pe, GI, [(0, turn(k, extra="max", ring_=(bank[0:2], S2, GAP2))), (1, conv_turn), (1, mix), (2, conv_root)])
                barrier(pe, "pe")

            pe.wait_ge(one["step_dve"], 4)
            for n, (filt, col) in enumerate(FEATS):
                for m, kk in enumerate(filt):
                    rows_out = C + 1 if kk == 0 else C
                    lhs = wh[0][0:C, (filt_at[n] + m) * (C + 1):(filt_at[n] + m) * (C + 1) + rows_out]
                    nc.tensor.matmul(bank[kk][0:rows_out, col:col + C], lhs, fus[0][0:C, n * C:(n + 1) * C],
                                     start=True, stop=True, skip_group_check=True)
            for kk in range(4):
                who = [n for n, (filt, _) in enumerate(FEATS) if kk in filt]
                rows_out = C + 1 if kk == 0 else C
                for x, n in enumerate(who):
                    s0 = (filt_at[n] + kk) * (C + 1)
                    last = nc.tensor.matmul(bank[4 + kk][0:rows_out, 0:3], wh[0][0:C, s0:s0 + rows_out], att[0][0:C, n * 3:n * 3 + 3],
                                            start=(x == 0), stop=(x == len(who) - 1))
            last.then_inc(one["step_pe"], 1)
            barrier(pe, "pe")

            for k, before in ((CHEB1, prescaled), (CHEB2, None)):
                scan_pass(k, before=before)
                barrier(pe, "pe")

            def f_turn(i, j, ch):
                for n in range(3):
                    x = 3 * cnt(i, j) + n
                    if n == 2:
                        pe.wait_ge(thirds, cnt(i, j) + 1)
                    elif n == 0:
                        pe.wait_ge(ld[j], LD["cheb3"] + 16 * (i + 1))
                    ge(pe, fcopied, x - FGAP[n] + 1)
                    for q in range(Q):
                        at_ = q * 3 * C + n * C
                        last = nc.tensor.transpose(bank[FBANK[n]][0:C, q * P:(q + 1) * P],
                                                   cheb_p[S3[j]][:, at_:at_ + C], ident[:, :])
                    last.then_inc(fturned, 1)

            def f_mix(i, j, ch):
                pe.wait_ge(fcopied, 3 * cnt(i, j) + 3)
                for q in range(Q):
                    ge(pe, fread, 4 * cnt(i, j) + q - 1)
                    for n in range(3):
                        last = nc.tensor.matmul(bank[6 + q % 2][:, 0:WIDE[n + 1]], cheb_t[S2[j] * 3 + n][0:C, q * P:(q + 1) * P],
                                                w_feat[n + 1][0:C, 0:WIDE[n + 1]], start=(n == 0), stop=(n == 2), skip_group_check=True)
                    last.then_inc(fmixed, 1)
            pe.sem_inc(fmixed, FCREDIT)
            pipeline(pe, GI, [(0, turn(CHEB3, ring_=(bank[0:2], S2, GAP2))), (0, turn_back(CHEB3, ring_=(bank[2:4], S2, GAP2))),
                              (1, f_turn), (1, f_mix)])
            barrier(pe, "pe")

            def a_turn(i, j, ch):
                pe.wait_ge(ld[j], LD["attend"] + 32 * (i + 1))
                ge(pe, dsem["attend", "copied"], cnt(i, j) - GAP2[j] + 1)
                for q in range(Q):
                    last = nc.tensor.transpose(bank[S2[j]][0:C, q * P:(q + 1) * P], a_x[j][:, q * C:q * C + C], ident[:, :])
                last.then_inc(dsem["attend", "turned"], 1)

            def a_mix(i, j, ch):
                pe.wait_ge(one["ones_set"], 3)
                pe.wait_ge(dsem["attend", "copied"], cnt(i, j) + 1)
                for q in range(Q):
                    if q % 2 == 0:
                        ge(pe, dsem["attend", "summed"], 2 * cnt(i, j) + q // 2 - 1)
                    last = nc.tensor.matmul(bank[2 + q][:, 0:FW], a_t[S3[j]][0:C + 1, q * P:(q + 1) * P], w_feat[0][0:C + 1, :],
                                            start=True, stop=True)
                    if q % 2:
                        last.then_inc(dsem["attend", "mixed2"], 1)

            def a_back(i, j, ch):
                pe.wait_ge(dsem["attend", "used"], cnt(i, j) + 1)
                ge(pe, dsem["attend", "final"], cnt(i, j) - GAP2[j] + 1)
                for q in range(Q):
                    last = nc.tensor.transpose(pmm[S2[j]][0:C, q * P:(q + 1) * P], a_h[j][:, q * C:q * C + C], ident[:, :])
                last.then_inc(dsem["attend", "turned2"], 1)
            pipeline(pe, TI, [(0, a_turn), (1, a_mix), (5, a_back)])
            barrier(pe, "pe")
            pe.wait_ge(one["step_dve"], 6)
            for n in range(2):
                last = nc.tensor.matmul(bank[0][:, n * C:(n + 1) * C], bn_wide[n][0:C, :], ident[0:C, 0:C], start=True, stop=True)
            last.then_inc(one["step_pe"], 1)
            barrier(pe, "pe")
            barrier(pe, "pe")

        @block.scalar
        def _(act):
            def stage(k, idx):
                def f(i, j, ch=None):
                    ge(act, taken, k * GROUPS + cnt(i, j) - R + 1)
                    nc.scalar.copy(get_st[:, j, :], idx[:, at(i, j, Q)]).then_inc(staged, 1)
                return f

            def finish(k, evacuate=True):
                def f(i, j, ch=None):
                    ge(act, put[j], PUT[k] + 64 * i)
                    nc.scalar.copy(put_st[:, j, :], put_i[:, at(i, j, Q)]).then_inc(put_ready, 1)
                    if evacuate:
                        act.wait_ge(tout, scans(k) * GROUPS + cnt(i, j) + 1)
                        nc.scalar.copy(out_r[:, j, :], pout[S3[j]][:, 0:QC]).then_inc(freed, 1)
                return f

            def stage_pass(k, idx):
                f = stage(k, idx)
                with act.Fori(0, GI) as i:
                    for j in range(R):
                        f(i, j)

            act.wait_ge(one["cleared"], 1)
            with act.Fori(0, TI) as i:
                part = agg_tab[bass.ds(i * (R * GRP), R * GRP), :].rearrange("(p q) c -> p (q c)", p=P)
                act.dma_start(part, zeros[0]).then_inc(one["zeroed"], 16)
            act.wait_ge(setup_ld, 16 * 11)
            act.wait_ge(one["puts"], 1)
            pipeline(act, GI, [(0, stage(SUM0, src_i)), (R, finish(SUM0))], peel=2)
            barrier(act, "act")
            act.wait_ge(one["step_dve"], 2)
            nc.scalar.activation(deg[7][0:TILES, :], deg[7][0:TILES, :], ACT.Sqrt).then_inc(one["step_act"], 1)
            nc.scalar.activation(deg[8][0:TILES, :], deg[8][0:TILES, :], ACT.Sqrt).then_inc(one["step_act"], 1)
            barrier(act, "act")

            def copied(ph, dst):
                def f(i, j, ch):
                    act.wait_ge(dsem[ph, "turned"], cnt(i, j) + 1)
                    ge(act, dsem[ph, "mixed1" if ph == "gin" else "mixed2"], cnt(i, j) - GAP3[j] + 1)
                    nc.scalar.copy(dst[S3[j]][0:C, :], pin[S3[j]][0:C, :]).then_inc(dsem[ph, "copied"], 1)
                return f

            def squares(ph, src, sq):
                def f(i, j, ch):
                    act.wait_ge(dsem[ph, "centred"], cnt(i, j) + 1)
                    if ph != "conv":
                        ge(act, dsem[ph, "reduced"], cnt(i, j) - GAP3[j] + 1)
                    nc.scalar.activation(sq[S3[j]], src[j], ACT.Square).then_inc(dsem[ph, "squared"], 1)
                return f

            def roots(ph, s, ready="reduced"):
                def f(i, j, ch):
                    act.wait_ge(dsem[ph, ready], cnt(i, j) + 1)
                    nc.scalar.activation(s[j][:, 3 * Q:4 * Q], s[j][:, 2 * Q:3 * Q], ACT.Sqrt, bias=eps_col[:, :], scale=1.0 / C).then_inc(dsem[ph, "rooted"], 1)
                return f

            def gin_relu(i, j, ch):
                act.wait_ge(dsem["gin", "mixed1"], cnt(i, j) + 1)
                ge(act, dsem["gin", "mixed2"], cnt(i, j) - GAP3[j] + 1)
                nc.scalar.activation(gin_h[S3[j]][0:C, :], pout[S3[j]][0:C, :], ACT.Relu, bias=b_gin1[0][0:C, :]).then_inc(dsem["gin", "relued"], 1)

            def squares_summed(ph, y, s, sq, bias):
                def f(i, j, ch):
                    act.wait_ge(dsem[ph, "centred"], cnt(i, j) + 1)
                    for q in range(Q):
                        last = nc.scalar.activation(sq[0][:, q * C:q * C + C], y[j][:, q * C:q * C + C], ACT.Square,
                                                    bias=s[j][:, Q + q:Q + q + 1] if bias else 0.0,
                                                    accum_out=s[j][:, 2 * Q + q:2 * Q + q + 1])
                    last.then_inc(dsem[ph, "squared"], 1)
                return f

            def gin_roots(i, j, ch):
                act.wait_ge(dsem["gin", "squared"], cnt(i, j) + 1)
                s_ = gin_s[j]
                nc.scalar.activation(s_[:, 3 * Q:4 * Q], s_[:, 2 * Q:3 * Q], ACT.Sqrt, bias=eps_col[:, :], scale=1.0 / C)
                nc.scalar.activation(s_[:, 4 * Q:5 * Q], s_[:, 2 * Q:3 * Q], ACT.Sqrt, bias=eps2_col[:, :], scale=(1.0 + EPS / 4) / C).then_inc(dsem["gin", "rooted"], 1)

            pipeline(act, TI, [(0, copied("gin", gin_r)), (1, gin_relu), (3, squares_summed("gin", gin_y, gin_s, gin_sq, False)), (3, gin_roots)])
            barrier(act, "act")
            stage_pass(DSTS, dst_i)
            stage_pass(HOP1, src_i)
            barrier(act, "act")
            def own_act(u, i, j):
                T = own_tile(u, i)
                if j in (1, 3):
                    act.wait_ge(dsem["own", "turned"], 2 * T + (j + 1) // 2)
                    act.wait_ge(dsem["own", "mixed"], 2 * T + 2)
                    nc.scalar.copy((n_t if j == 1 else n_t2)[0:C, :], pmm[0][0:C, :]).then_inc(dsem["own", "copied"], 1)
                if j == 4:
                    act.wait_ge(dsem["own", "centred"], T + 1)
                    nc.scalar.activation(n_sq, n_y, ACT.Square).then_inc(dsem["own", "squared"], 1)
                if j == 5:
                    act.wait_ge(dsem["own", "reduced"], T + 1)
                    nc.scalar.activation(hop_s[0][:, 3 * Q:4 * Q], hop_s[0][:, 2 * Q:3 * Q], ACT.Sqrt, bias=eps_col[:, :], scale=1.0 / C).then_inc(dsem["own", "rooted"], 1)
            act.sem_inc(dsem["own", "copied"], 2)
            with act.Fori(0, ROUNDS) as r:
                for h in range(2):
                    act.wait_ge(table_written, r * 2 + (h + 1))
                    f = stage(r * 2 + (HOP2 + h), hop_i[h])
                    for j in range(R):
                        f(0, j)
                    with act.Fori(0, GI - 1) as i:
                        for j in range(R):
                            f(i + 1, j)
                            own_act(r * 2 + h, i, j)
                    for j in range(R):
                        own_act(r * 2 + h, GI - 1, j)
            act.wait_ge(table_written, HOPS - 1)
            act.wait_ge(own_c, 16 * (TILES + 1))
            act.wait_ge(own_x, 16 * (TILES + 1))

            def hopl_squares(i, j, ch=None):
                act.wait_ge(dsem["hopl", "centred"], cnt(i, j) + 1)
                ge(act, wr[j], WR["x2_slot"] + 16 * i)
                for q in range(Q):
                    last = nc.scalar.activation(out_r[:, j, q * C:q * C + C], state[:, at(i, j, QC, C, q * C)], ACT.Square,
                                                accum_out=hop_s[j][:, 2 * Q + q:2 * Q + q + 1])
                last.then_inc(dsem["hopl", "squared"], 1)
            pipeline(act, GI, [(0, stage(HOPL, hop_i[0])), (R, hopl_squares), (R, roots("hopl", hop_s, "squared"))])
            barrier(act, "act")
            for n, k in enumerate((MAX1, MAX2)):
                def conv_copied(i, j, ch=None):
                    act.wait_ge(dsem["conv", "turned"], n * GROUPS + cnt(i, j) + 1)
                    nc.scalar.copy(d_t[S3[j]][0:C, :], bank[2][0:C, :]).then_inc(dsem["conv", "copied"], 1)
                def negs(i, j, ch=None):
                    nc.scalar.activation(neg[0:C, at(i, j, GRP)], keep[0:C, at(i, j, GRP)], ACT.Copy, scale=BIG, bias=-BIG).then_inc(negated, 1)
                head = [] if n else [(R - 1, negs)]
                tail = [(R, finish(k, evacuate=False)), (R, squares("conv", d_y, d_sq)), (R, roots("conv", d_s))] if n else []
                pipeline(act, GI, [(0, stage(k, hop_i[0]))] + head + [(R - 1, conv_copied)] + tail)
                barrier(act, "act")
            barrier(act, "act", passing=True)
            stage_pass(CHEB1, src_i)
            barrier(act, "act")
            stage_pass(CHEB2, q_i)
            barrier(act, "act")

            def f_copied(i, j, ch):
                for n in range(3):
                    act.wait_ge(fturned, 3 * cnt(i, j) + n + 1)
                    act.wait_ge(fmixed, FCREDIT + 4 * (cnt(i, j) - GAP2[j] + 1))
                    nc.scalar.copy(cheb_t[S2[j] * 3 + n][0:C, :], bank[FBANK[n]][0:C, :]).then_inc(fcopied, 1)
            pipeline(act, GI, [(0, stage(CHEB3, q_i)), (R, finish(CHEB3, evacuate=False)), (R - 1, f_copied)])
            barrier(act, "act")

            def a_copied(i, j, ch):
                ge(act, dsem["attend", "turned2"], cnt(i, j) - R + 1)
                act.wait_ge(dsem["attend", "turned"], cnt(i, j) + 1)
                ge(act, dsem["attend", "mixed2"], 2 * (cnt(i, j) - GAP3[j] + 1))
                nc.scalar.copy(a_t[S3[j]][0:C, :], bank[S2[j]][0:C, :]).then_inc(dsem["attend", "copied"], 1)

            def a_scaled(i, j, ch):
                act.wait_ge(dsem["attend", "scaled"], cnt(i, j) + 1)
                ge(act, st[j], ST["attend"] + 16 * i)
                for q in range(Q):
                    e = a_s[j][:, Q + 3 * q + 2:Q + 3 * q + 3]
                    nc.scalar.activation(a_h[j][:, q * C:q * C + C], a_f[j][:, q * FW:q * FW + C], ACT.Copy, scale=e)
                    e, col = a_s[j][:, Q + 3 * q + 1:Q + 3 * q + 2], q * FW + FEATS[1][1]
                    ins = nc.scalar.activation(a_f[j][:, col:col + C], a_f[j][:, col:col + C], ACT.Copy, scale=e)
                ins.then_inc(dsem["attend", "shared"], 1)

            def a_exp(i, j, ch):
                act.wait_ge(dsem["attend", "topped"], cnt(i, j) + 1)
                nc.scalar.activation(a_s[j][:, Q:4 * Q], a_s[j][:, Q:4 * Q], ACT.Exp).then_inc(dsem["attend", "raised"], 1)
            pipeline(act, TI, [(0, a_copied), (1, a_exp), (2, a_scaled)])
            barrier(act, "act")
            act.wait_ge(one["step_dve"], 5)
            nc.scalar.activation(bn[0][0:C, 2:3], bn[0][0:C, 1:2], ACT.Sqrt, bias=eps_col[0:C, :]).then_inc(one["step_act"], 1)
            barrier(act, "act")

            def norm_roots(i, j, ch):
                act.wait_ge(dsem["norm", "squared"], cnt(i, j) + 1)
                nc.scalar.activation(d_s[j][:, 3 * Q:4 * Q], d_s[j][:, 2 * Q:3 * Q], ACT.Sqrt, bias=eps_col[:, :], scale=1.0 / C).then_inc(dsem["norm", "rooted"], 1)

            pipeline(act, TI, [(0, squares_summed("norm", d_y, d_s, d_sq, True)), (0, norm_roots)])
            barrier(act, "act")

        @block.vector
        def _(dve):
            V = nc.vector
            ch = straight(dve, "dve")
            V.memset(zeros[0], 0.0)
            V.memset(zero_row[:, :], 0.0)
            V.memset(eps_col[:, :], EPS)
            V.memset(eps2_col[:, :], EPS * EPS / 4)
            V.memset(gin_h[0][C:C + 1, :], 1.0)
            V.memset(gin_h[1][C:C + 1, :], 1.0)
            V.memset(gin_h[2][C:C + 1, :], 1.0)
            for j in range(R):
                V.memset(gin_a[j], 0.0)
            ch.step(V.memset(sc[:, :, :], 0.0))
            dve.sem_inc(one["cleared"], 1)
            dve.wait_ge(setup_ld, 16 * 11)
            flag = tmp[:, 0, 0:IDX]
            digit = tmp[:, 1, 0:IDX].bitcast(I32)
            ch.step(V.tensor_tensor(flag, dst_i[:, :], put_i[:, :], ALU.is_equal))
            ch.step(V.scalar_tensor_tensor(put_i[:, :], flag, float(FAR), dst_i[:, :], ALU.mult, ALU.add))
            dve.sem_inc(one["puts"], 1)
            for n, a in enumerate((src_i, dst_i)):
                ch.step(V.tensor_scalar(digit, a[:, :], GRP - 1, None, ALU.bitwise_and))
                ch.step(V.tensor_copy(lo_hi[:, 2 * n, :], digit))
                ch.step(V.tensor_scalar(digit, a[:, :], GRP.bit_length() - 1, None, ALU.logical_shift_right))
                ch.step(V.tensor_copy(lo_hi[:, 2 * n + 1, :], digit))
            end_straight(ch, "dve")
            dve.wait_ge(one["idents"], 1)

            def keep_flags(i, j, ch):
                dve.wait_ge(ld[j], LD["keep"] + 16 * (i + 1))
                row = keep_ld[j].bitcast(I32)
                V.tensor_tensor(keep[0:C, at(i, j, GRP)], row[0:C, 1:GRP + 1], row[0:C, 0:GRP], ALU.is_equal).then_inc(keeps, 1)

            def onehots(i, j, ch):
                for q in range(Q):
                    ge(dve, one["histed"], 4 * cnt(i, j) + q - 3)
                    row = onehot[q].bitcast(F16).rearrange("p (k n) -> p k n", k=2)
                    for n in range(2):
                        V.tensor_scalar(row[:, n, 0:GRP], iota_lo[0].bitcast(F16), lo_hi[:, 2 * n, at(i, j, Q, 1, q)], None, ALU.is_equal)
                        last = V.tensor_scalar(row[:, n, GRP:GRP + P], iota_hi[0].bitcast(F16), lo_hi[:, 2 * n + 1, at(i, j, Q, 1, q)], None, ALU.is_equal)
                    last.then_inc(one["hot"], 1)

            def scan(k, mask=None, banks=pin, S=S3):

                def f(i, j, ch=None):
                    g = scans(k) * GROUPS + cnt(i, j)
                    if mask is None:
                        dve.wait_ge(taken, k * GROUPS + cnt(i, j) + 1)
                        src, m, ops = banks[S[j]][0:C, :], keep[0:C, at(i, j, GRP)], (ALU.mult, ALU.add)
                    else:
                        dve.wait_ge(mixed, (k - MAX1) * GROUPS + cnt(i, j) + 1)
                        dve.wait_ge(negated, cnt(i, j) + 1 if k == MAX1 else GROUPS)
                        src, m, ops = pmm[S2[j]][0:C, :], mask[0:C, at(i, j, GRP)], (ALU.add, ALU.max)
                    if isinstance(k, int) and k == SUM0:
                        dve.wait_ge(keeps, cnt(i, j) + 1)
                    ge(dve, tout, g - GAP3[j] + 1)
                    ge(dve, scanned, g)
                    V.tensor_tensor_scan(sc[0:C, S3[j], :], m, src, sc[0:C, S3[j - 1], GRP - 1:GRP], *ops).then_inc(scanned, 1)
                return f

            pipeline(dve, GI, [(0, keep_flags), (0, onehots), (0, scan(SUM0))])
            barrier(dve, "dve")

            ch = straight(dve, "dve")
            D = [d[0:TILES, :] for d in deg]
            h_out, h_in, cum, one_, off, f_in, slot_map, s_in, s_out, node = D
            V.memset(one_, 1.0)
            V.tensor_copy(h_out, pmm[0][0:TILES, :])
            ch.step(V.tensor_copy(h_in, pmm[1][0:TILES, :]))
            ch.step(V.tensor_tensor_scan(cum, one_, h_in, 0.0, ALU.mult, ALU.add))
            dve.sem_inc(one["step_dve"], 1)
            V.tensor_scalar(f_in, h_in, 1.0, None, ALU.min)
            V.tensor_scalar(s_in, h_in, 1.0, None, ALU.add)
            V.tensor_scalar(s_out, h_out, 1.0, None, ALU.max)
            ch.step(V.tensor_scalar(h_out, h_out, 1.0, None, ALU.min))
            dve.wait_ge(one["step_pe"], 1)
            ch.step(V.tensor_copy(off[:, 0:1], bank[0][0:TILES, 0:1]))
            ch.step(V.tensor_scalar(slot_map, cum, off[:, 0:1], float(NP - 1), ALU.add, ALU.add))
            ch.step(V.tensor_tensor(slot_map, slot_map, node, ALU.subtract))
            ch.step(V.tensor_tensor(slot_map, slot_map, f_in, ALU.mult))
            ch.step(V.tensor_tensor(slot_map, slot_map, node, ALU.add))
            dve.sem_inc(one["step_dve"], 1)
            dve.wait_ge(one["step_act"], 2)
            ch.step(V.reciprocal(s_in, s_in))
            ch.step(V.reciprocal(s_out, s_out))
            ch.step(V.tensor_tensor(s_out, s_out, h_out, ALU.mult))
            dve.sem_inc(one["step_dve"], 1)
            dve.wait_ge(one["step_pe"], 2)
            for n in range(3):
                last = V.tensor_copy(node_sc[:, n, :].rearrange("p (t q) -> p q t", q=Q),
                                     bank[3 + n][:, 0:Q * TILES].rearrange("p (q t) -> p q t", q=Q))
            ch.step(last)
            end_straight(ch, "dve")
            barrier(dve, "dve")

            def centre(ph, y, s, ch, j, sem_):
                ch.step(V.tensor_reduce(s[j][:, 0:Q], v3(y[j]), AX.X, ALU.add))
                ch.step(V.tensor_scalar(s[j][:, Q:2 * Q], s[j][:, 0:Q], -1.0 / C, None, ALU.mult))
                V.tensor_tensor(v3(y[j]), v3(y[j]), spread(s[j][:, Q:2 * Q]), ALU.add).then_inc(dsem[ph, "centred"], 1)

            def reduce(ph, sq, s):
                def f(i, j, ch):
                    dve.wait_ge(dsem[ph, "squared"], cnt(i, j) + 1)
                    V.tensor_reduce(s[j][:, 2 * Q:3 * Q], v3(sq[S3[j]]), AX.X, ALU.add).then_inc(dsem[ph, "reduced"], 1)
                return f

            def scaled(ph, y, s, ch, i, j, out, nst):
                dve.wait_ge(dsem[ph, "rooted"], cnt(i, j) + 1)
                n = 2 if ph == "gin" else 1
                r_ = (5 if ph == "gin" else 0) * Q
                ch.step(V.reciprocal(s[j][:, r_:r_ + n * Q], s[j][:, 3 * Q:(3 + n) * Q]))
                ge(dve, st[j], ST[ph] + 16 * nst * i)
                return V.tensor_tensor(v3(out[j]), v3(y[j]), spread(s[j][:, r_:r_ + Q]), ALU.mult)

            def gin_res(i, j, ch):
                dve.wait_ge(dsem["gin", "mixed2"], cnt(i, j) + 1)
                V.tensor_tensor(gin_y[j], pmm[S2[j]][:, 0:QC], gin_x[j], ALU.add).then_inc(dsem["gin", "used"], 1)
                dve.wait_ge(dsem["gin", "used"], cnt(i, j) + 1)
                centre("gin", gin_y, gin_s, ch, j, None)

            def gin_out(i, j, ch):
                scaled("gin", gin_y, gin_s, ch, i, j, gin_o, 3)
                V.tensor_tensor(v3(gin_u[j]), v3(gin_y[j]), spread(gin_s[j][:, 6 * Q:7 * Q]), ALU.mult).then_inc(dsem["gin", "final"], 1)
            pipeline(dve, TI, [(3, gin_res), (4, gin_out)], "dve", steps=R * 3)
            barrier(dve, "dve")

            def dst_rows(i, j):
                dve.wait_ge(got[j], 64 * (DSTS * GI + i + 1))
                row = v3(G[:, j, :], TW)
                V.tensor_copy(sd_in[:, at(i, j, Q)], row[:, :, C + 1])
                V.tensor_copy(w_out[:, at(i, j, Q)], row[:, :, C + 2])
                V.tensor_copy(v3(g0[:, at(i, j, QC)]), row[:, :, 0:C]).then_inc(taken, 1)
            with dve.Fori(0, GI) as i:
                for j in range(R):
                    dst_rows(i, j)
            ch = straight(dve, "dve")
            dve.wait_ge(taken, (DSTS + 1) * GROUPS)
            ch.step(V.tensor_tensor(w_hop[:, :], sd_in[:, :], sd_in[:, :], ALU.mult))
            ch.step(V.tensor_scalar(w_hop[:, :], w_hop[:, :], KEEP, None, ALU.mult))
            ch.step(V.reciprocal(sd_in[:, :], sd_in[:, :]))
            end_straight(ch, "dve")

            def own_dve(u, i, j, ch):
                T, s_ = own_tile(u, i), hop_s[0]
                if j == 2:
                    dve.wait_ge(dsem["own", "mixed"], 2 * T + 3)
                    dve.wait_ge(own_c, 16 * T + 16)
                    ch.step(V.tensor_scalar(n_c, pmm[1][:, 0:QC], 0.01, None, ALU.mult))
                    V.tensor_tensor(n_c, pmm[1][:, 0:QC], n_c, ALU.max).then_inc(dsem["own", "leaked"], 1)
                if j == 4:
                    dve.wait_ge(dsem["own", "mixed"], 2 * T + 4)
                    dve.wait_ge(own_x, 16 * T + 16)
                    ch.step(V.tensor_scalar(n_y, pmm[1][:, 0:QC], 0.01, None, ALU.mult))
                    ch.step(V.tensor_tensor(n_y, pmm[1][:, 0:QC], n_y, ALU.max))
                    V.tensor_tensor(n_y, n_y, n_x, ALU.add).then_inc(dsem["own", "summed"], 1)
                    dve.wait_ge(dsem["own", "summed"], T + 2)
                    ch.step(V.tensor_reduce(s_[:, 0:Q], v3(n_y), AX.X, ALU.add))
                    ch.step(V.tensor_scalar(s_[:, Q:2 * Q], s_[:, 0:Q], -1.0 / C, None, ALU.mult))
                    V.tensor_tensor(v3(n_y), v3(n_y), spread(s_[:, Q:2 * Q]), ALU.add).then_inc(dsem["own", "centred"], 1)
                if j == 5:
                    dve.wait_ge(dsem["own", "squared"], T + 1)
                    V.tensor_reduce(s_[:, 2 * Q:3 * Q], v3(n_sq), AX.X, ALU.add).then_inc(dsem["own", "reduced"], 1)
                if j == 6:
                    dve.wait_ge(dsem["own", "rooted"], T + 1)
                    ch.step(V.reciprocal(s_[:, 0:Q], s_[:, 3 * Q:4 * Q]))
                    V.tensor_tensor(v3(n_y), v3(n_y), spread(s_[:, 0:Q]), ALU.mult).then_inc(dsem["own", "final"], 1)
            OWN_STEPS = 6

            def hop(k, old, last=False):
                def sources(i, j, ch):
                    ge(dve, got[j], 64 * (HOP1 * GI + i + 1))
                    V.tensor_copy(w_src[:, at(i, j, Q)], v3(G[:, j, :], TW)[:, :, C + 2])
                    V.tensor_copy(hop_i[0][:, at(i, j, Q)], v3(G[:, j, :], TW)[:, :, C]).then_inc(moved, 1)

                def f(i, j, ch):
                    g = scans(k) * GROUPS + cnt(i, j)
                    dve.wait_ge(tout, g + 1)
                    a, b = tmp[:, S3[j], :], at(i, j, QC)
                    V.tensor_tensor(a, pout[S3[j]][:, 0:QC], old[:, b], ALU.add).then_inc(freed, 1)
                    dve.wait_ge(freed, g + 1)
                    ch.step(V.tensor_tensor(v3(a), v3(a), spread(w_hop[:, at(i, j, Q)]), ALU.mult))
                    if not last:
                        V.scalar_tensor_tensor(state[:, b], g0[:, b], ALPHA, a, ALU.mult, ALU.add).then_inc(done, 1)
                    else:
                        ch.step(V.scalar_tensor_tensor(a, g0[:, b], ALPHA + 1.0, a, ALU.mult, ALU.add))
                        ch.step(V.tensor_tensor(v3(a), v3(a), spread(sd_in[:, at(i, j, Q)]), ALU.mult))
                        ch.step(V.tensor_reduce(hop_s[j][:, 0:Q], v3(a), AX.X, ALU.add))
                        ch.step(V.tensor_scalar(hop_s[j][:, Q:2 * Q], hop_s[j][:, 0:Q], -1.0 / C, None, ALU.mult))
                        V.tensor_tensor(v3(state[:, b]), v3(a), spread(hop_s[j][:, Q:2 * Q]), ALU.add).then_inc(dsem["hopl", "centred"], 1)
                if old is g0:
                    return [(0, sources), (1, scan(k)), (2, f)]
                return [(0, scan(k)), (1, f)]

            def hop_pass(k, old, start, steps=R, u=None):
                own = [(0, lambda i, j, ch: own_dve(u, i, j, ch))] if u is not None else []
                pipeline(dve, GI, hop(k, old) + own, "dve", steps=steps, start=start)
            hop_pass(HOP1, g0, chain_at["dve"])
            chain_at["dve"] += R * GI
            ch = straight(dve, "dve")
            dve.wait_ge(moved, GROUPS)
            dve.wait_ge(done, GROUPS)
            ch.step(V.tensor_scalar(flag, hop_i[0][:, :], float(NP), None, ALU.is_ge))
            ch.step(V.scalar_tensor_tensor(hop_i[1][:, :], flag, float(EP), hop_i[0][:, :], ALU.mult, ALU.add))
            ch.step(V.tensor_scalar(digit, hop_i[0][:, :], float(NP + EP), None, ALU.subtract))
            ch.step(V.tensor_tensor(digit, digit, flag, ALU.mult))
            ch.step(V.tensor_scalar(q_i[:, :], digit, float(EP), None, ALU.add))
            V.memset(n_t[C:C + 1, :], 1.0)
            ch.step(V.memset(n_t2[C:C + 1, :], 1.0))
            end_straight(ch, "dve")
            barrier(dve, "dve")
            for s_, n in ((dsem["own", "summed"], 1), (own_c, 16), (own_x, 16)):
                dve.sem_inc(s_, n)
            per = R + OWN_STEPS
            with dve.Fori(0, ROUNDS) as r:
                for h in range(2):
                    hop_pass(r * 2 + (HOP2 + h), state, r * (2 * per * GI) + (chain_at["dve"] + h * per * GI), steps=per, u=r * 2 + h)
            chain_at["dve"] += ROUNDS * 2 * per * GI

            def hopl_out(i, j, ch):
                dve.wait_ge(dsem["hopl", "rooted"], cnt(i, j) + 1)
                ch.step(V.reciprocal(hop_s[j][:, 0:Q], hop_s[j][:, 3 * Q:4 * Q]))
                V.tensor_tensor(v3(out_r[:, j, :]), v3(state[:, at(i, j, QC)]), spread(hop_s[j][:, 0:Q]), ALU.mult).then_inc(outdone, 1)

            pipeline(dve, GI, hop(HOPL, state, True) + [(2, hopl_out)], "dve", steps=6 * R)
            barrier(dve, "dve")

            for n in range(3):
                V.memset(d_t[n][C:C + 1, :], 1.0)
            dve.drain().then_inc(one["cleared"], 1)

            for n, k in enumerate((MAX1, MAX2)):
                def move(i, j, ch):
                    g = n * GROUPS + cnt(i, j)
                    dve.wait_ge(taken, k * GROUPS + cnt(i, j) + 1)
                    ge(dve, mixed, g - GAP3[j] + 1)
                    V.tensor_copy(mix_r[S3[j]][0:C, :], bank[S2[j]][0:C, :]).then_inc(moved, 1)

                def conv_res(i, j, ch):
                    dve.wait_ge(tout, scans(k) * GROUPS + cnt(i, j) + 1)
                    if n == 0:
                        ge(dve, wr[j], WR["c1_slot"] + 16 * i)
                    dst = d_y[j] if n else out_rows[j]
                    src = pout[S3[j]][:, 0:QC]
                    ch.step(V.tensor_scalar(dst, src, 0.01, None, ALU.mult))
                    V.tensor_tensor(dst, src, dst, ALU.max).then_inc(freed, 1)
                    dve.wait_ge(freed, scans(k) * GROUPS + cnt(i, j) + 1)
                    if n == 0:
                        dve.sem_inc(outdone, 1)
                    else:
                        dve.wait_ge(ld[j], LD["max2"] + 16 * nload["max2"] * (i + 1))
                        ch.step(V.tensor_tensor(dst, dst, d_w[j], ALU.add))
                        centre("conv", d_y, d_s, ch, j, None)

                def conv_out(i, j, ch):
                    dve.wait_ge(dsem["conv", "rooted"], cnt(i, j) + 1)
                    ch.step(V.reciprocal(d_s[j][:, 0:Q], d_s[j][:, 3 * Q:4 * Q]))
                    dve.wait_ge(put_ready, KU[k] * GROUPS + cnt(i, j) + 1)
                    V.tensor_tensor(v3(out_rows[j]), v3(d_y[j]), spread(d_s[j][:, 0:Q]), ALU.mult).then_inc(outdone, 1)
                if n:
                    pipeline(dve, GI, [(3, reduce("conv", d_sq, d_s)), (0, move), (1, scan(k, mask=neg)), (2, conv_res), (4, conv_out)],
                             "dve", steps=R * 5)
                else:
                    pipeline(dve, GI, [(0, move), (1, scan(k, mask=neg)), (2, conv_res)], "dve", steps=R)
                barrier(dve, "dve")

            ch = straight(dve, "dve")
            dve.wait_ge(one["prep_ld"], 16 * 11)
            W = lambda n, m: wt[0][0:C, (filt_at[n] + m) * C:(filt_at[n] + m + 1) * C]
            H = lambda n, m: wh[0][0:C, (filt_at[n] + m) * (C + 1):(filt_at[n] + m) * (C + 1) + C]
            V.tensor_copy(H(0, 0), W(0, 0))
            V.tensor_scalar(H(0, 1), W(0, 1), -1.0, None, ALU.mult)
            V.tensor_tensor(H(1, 0), W(1, 0), W(1, 2), ALU.subtract)
            V.tensor_scalar(H(1, 1), W(1, 1), -1.0, None, ALU.mult)
            V.tensor_scalar(H(1, 2), W(1, 2), 2.0, None, ALU.mult)
            V.tensor_tensor(H(2, 0), W(2, 0), W(2, 2), ALU.subtract)
            V.tensor_tensor(H(2, 1), W(2, 3), W(2, 1), ALU.subtract)
            V.tensor_scalar(H(2, 2), W(2, 2), 2.0, None, ALU.mult)
            V.tensor_scalar(H(2, 3), W(2, 3), 2.0, None, ALU.mult)
            for n in range(3):
                c = filt_at[n] * (C + 1) + C
                last = V.tensor_copy(wh[0][0:C, c:c + 1], wb[0][0:C, n:n + 1])
            ch.step(last)
            dve.sem_inc(one["step_dve"], 1)
            dve.wait_ge(one["step_pe"], 3)
            for kk in range(4):
                kr = C + 1 if kk == 0 else C
                V.tensor_copy(w_feat[kk][0:kr, LOGIT:LOGIT + 3], bank[4 + kk][0:kr, 0:3])
                V.tensor_copy(w_feat[kk][0:kr, 0:C], bank[kk][0:kr, 0:C])
                if WIDE[kk] > C + 3:
                    ch.step(V.tensor_copy(w_feat[kk][0:kr, C + 3:WIDE[kk]], bank[kk][0:kr, C + 3:WIDE[kk]]))
            ch.step(V.tensor_tensor(w_feat[0][C:C + 1, :], w_feat[0][C:C + 1, :], att_b[0][C:C + 1, :], ALU.add))
            end_straight(ch, "dve")
            barrier(dve, "dve")
            for n, k in enumerate((CHEB1, CHEB2)):
                sc_f = scan(k)

                def cheb(i, j, ch):
                    g = scans(k) * GROUPS + cnt(i, j)
                    dve.wait_ge(tout, g + 1)
                    ge(dve, wr[j], WR["cheb1" if n == 0 else "cheb2"] + 32 * i)
                    w = spread(w_out[:, at(i, j, Q)])
                    V.tensor_tensor(v3(cheb_a[j]), v3(pout[S3[j]][:, 0:QC]), w, ALU.mult).then_inc(freed, 1)
                    dve.wait_ge(freed, g + 1)
                    V.tensor_tensor(v3(cheb_b[j]), v3(cheb_a[j]), w, ALU.mult).then_inc(done, 1)

                def prescale(i, j, ch):
                    dve.wait_ge(got[j], 64 * (CHEB1 * GI + i + 1))
                    row = v3(G[:, j, 0:QC])
                    V.tensor_tensor(row, row, spread(w_src[:, at(i, j, Q)]), ALU.mult).then_inc(prescaled, 1)
                pipeline(dve, GI, [(0, prescale), (1, sc_f), (2, cheb)] if n == 0 else [(0, sc_f), (1, cheb)])
                barrier(dve, "dve")


            def cheb_last(i, j, ch):
                g = scans(CHEB3) * GROUPS + cnt(i, j)
                dve.wait_ge(tout, g + 1)
                a, b = tmp[:, S3[j], :], v3(cheb_p[S3[j]], 3 * C)
                V.tensor_tensor(v3(a), v3(bank[2 + S2[j]][:, 0:QC]), spread(w_out[:, at(i, j, Q)]), ALU.mult).then_inc(freed, 1)
                dve.wait_ge(freed, g + 1)
                dve.wait_ge(ld[j], LD["cheb3"] + 16 * (i + 1))
                V.scalar_tensor_tensor(b[:, :, 2 * C:3 * C], v3(a), -2.0, b[:, :, 0:C], ALU.mult, ALU.add).then_inc(thirds, 1)

            def f_rows(i, j, ch):
                dve.wait_ge(put_ready, KU[CHEB3] * GROUPS + cnt(i, j) + 1)
                for q in range(Q):
                    dve.wait_ge(fmixed, FCREDIT + 4 * cnt(i, j) + q + 1)
                    V.tensor_copy(cheb_f[j][:, q * FW:(q + 1) * FW], bank[6 + q % 2][:, 0:FW]).then_inc(fread, 1)
            pipeline(dve, GI, [(0, scan(CHEB3, banks=bank[0:2], S=S2)), (0, cheb_last), (1, f_rows)])
            barrier(dve, "dve")
            for s_ in range(3):
                V.memset(a_t[s_][C:C + 1, :], 1.0).then_inc(one["ones_set"], 1)

            wide = ps[:, 2:2 + Q, :]

            def a_sum(i, j, ch):
                s_, f_ = a_s[j], v3(a_f[j], FW)
                logit = f_[:, :, LOGIT:LOGIT + 3]
                e3 = s_[:, Q:4 * Q].rearrange("p (q k) -> p q k", k=3)
                for n in range(2):
                    half = slice(2 * n, 2 * n + 2)
                    dve.wait_ge(dsem["attend", "mixed2"], 2 * cnt(i, j) + n + 1)
                    V.tensor_tensor(f_[:, half, :], wide[:, half, 0:FW], f_[:, half, :], ALU.add).then_inc(dsem["attend", "summed"], 1)
                dve.wait_ge(dsem["attend", "summed"], 2 * cnt(i, j) + 2)
                ch.step(V.tensor_reduce(s_[:, 0:Q], logit, AX.X, ALU.max))
                V.tensor_tensor(e3, logit, s_[:, 0:Q].unsqueeze(2).to_broadcast([P, Q, 3]), ALU.subtract).then_inc(dsem["attend", "topped"], 1)

            def a_soft(i, j, ch):
                s_ = a_s[j]
                e3 = s_[:, Q:4 * Q].rearrange("p (q k) -> p q k", k=3)
                dve.wait_ge(dsem["attend", "raised"], cnt(i, j) + 1)
                ch.step(V.tensor_reduce(s_[:, 4 * Q:5 * Q], e3, AX.X, ALU.add))
                ch.step(V.reciprocal(s_[:, 4 * Q:5 * Q], s_[:, 4 * Q:5 * Q]))
                V.tensor_tensor(e3, e3, s_[:, 4 * Q:5 * Q].unsqueeze(2).to_broadcast([P, Q, 3]), ALU.mult).then_inc(dsem["attend", "scaled"], 1)

            def a_fuse(i, j, ch):
                dve.wait_ge(dsem["attend", "joined"], cnt(i, j) + 1)
                col = FEATS[0][1]
                V.tensor_tensor(v3(a_h[j]), v3(a_h[j]), v3(a_f[j], FW)[:, :, col:col + C], ALU.add).then_inc(dsem["attend", "used"], 1)

            def a_stats(i, j, ch):
                dve.wait_ge(dsem["attend", "turned2"], cnt(i, j) + 1)
                V.bn_stats(stats[0][0:C, at(i, j, 6)], pmm[S2[j]][0:C, :]).then_inc(dsem["attend", "final"], 1)
            pipeline(dve, TI, [(4, a_fuse), (6, a_stats), (2, a_soft), (1, a_sum)], "dve", steps=R * 3)
            ch = straight(dve, "dve")
            real = (N - (TILES - 1) * GRP) // Q
            dve.wait_ge(dsem["attend", "final"], TILES)
            ch.step(V.bn_stats(stats[0][0:C, (TILES - 1) * 6:TILES * 6], pmm[S2[R - 1]][0:C, :].rearrange("c (q p) -> c q p", q=Q)[:, :, 0:real]))
            end_straight(ch, "dve")
            barrier(dve, "dve")
            ch = straight(dve, "dve")
            b_ = bn[0][0:C, :]
            ch.step(V.bn_aggr(b_[:, 0:2], stats[0][0:C, :]))
            dve.sem_inc(one["step_dve"], 1)
            dve.wait_ge(one["step_act"], 3)
            ch.step(V.reciprocal(b_[:, 3:4], b_[:, 2:3]))
            ch.step(V.tensor_tensor(b_[:, 6:7], b_[:, 3:4], b_[:, 4:5], ALU.mult))
            ch.step(V.tensor_tensor(b_[:, 7:8], b_[:, 0:1], b_[:, 6:7], ALU.mult))
            ch.step(V.tensor_tensor(b_[:, 7:8], b_[:, 5:6], b_[:, 7:8], ALU.subtract))
            V.tensor_copy(bn_wide[0][0:C, :], b_[:, 6:7].to_broadcast([C, P]))
            ch.step(V.tensor_copy(bn_wide[1][0:C, :], b_[:, 7:8].to_broadcast([C, P])))
            dve.sem_inc(one["step_dve"], 1)
            dve.wait_ge(one["step_pe"], 4)
            ch.step(V.tensor_copy(bn_row[0], bank[0][:, 0:2 * C]))
            end_straight(ch, "dve")
            barrier(dve, "dve")

            def norm_res(i, j, ch):
                dve.wait_ge(dsem["norm", "shifted"], cnt(i, j) + 1)
                V.scalar_tensor_tensor(d_y[j], d_z[j], 0.0, d_x[j], ALU.max, ALU.add).then_inc(dsem["norm", "used"], 1)
                dve.wait_ge(dsem["norm", "used"], cnt(i, j) + 1)
                ch.step(V.tensor_reduce(d_s[j][:, 0:Q], v3(d_y[j]), AX.X, ALU.add))
                V.tensor_scalar(d_s[j][:, Q:2 * Q], d_s[j][:, 0:Q], -1.0 / C, None, ALU.mult).then_inc(dsem["norm", "centred"], 1)

            def norm_out(i, j, ch):
                dve.wait_ge(dsem["norm", "rooted"], cnt(i, j) + 1)
                ch.step(V.reciprocal(d_s[j][:, 0:Q], d_s[j][:, 3 * Q:4 * Q]))
                ge(dve, st[j], ST["norm"] + 16 * i)
                for q in range(Q):
                    last = V.tensor_scalar(d_o[j][:, q * C:q * C + C], d_y[j][:, q * C:q * C + C],
                                           d_s[j][:, Q + q:Q + q + 1], d_s[j][:, q:q + 1], ALU.add, ALU.mult)
                last.then_inc(dsem["norm", "final"], 1)
            pipeline(dve, TI, [(0, norm_res), (2, norm_out)], "dve", steps=R * 2)
            barrier(dve, "dve")


def kernel(**inp):
    import numpy as np
    import concourse.bacc as bacc
    from concourse.bass_utils import run_bass_kernel_spmd as run

    nc = bacc.Bacc("TRN2", target_bir_lowering=False, num_devices=1, dynamic_dma_scratch_size=8192)
    a = {k: np.asarray(v) for k, v in inp.items()}
    f = np.float32

    def padded(v, n, fill, front=()):
        out = np.full((len(front) + n,) + v.shape[1:], fill, v.dtype)
        if front:
            out[:len(front)] = front
        out[len(front):len(front) + len(v)] = v
        return out

    arrays = {
        "x": padded(a["x"], NP, 0),
        "src": padded(a["src"], EP, N),
        "dst": padded(a["dst"], EP + 1, N, front=(-1,)),
        "edge_t": np.ascontiguousarray(padded(a["edge_attr_32"], EP, 0).T),
        "gin_w1": a["L0_gnn_W1"], "gin_b1": a["L0_gnn_b1"], "gin_w2": a["L0_gnn_W2"], "gin_b2": a["L0_gnn_b2"],
        "cheb_w": np.concatenate([w.T for n in (2, 3, 4) for w in a[f"L3_gnn_w{n}"]], axis=1),
        "cheb_b": np.stack([a[f"L3_gnn_b{n}"] for n in (2, 3, 4)], axis=1),
        "att_w": a["L3_gnn_attn_w"].reshape(3, C, 3).transpose(1, 0, 2).reshape(C, 9),
        "att_b": np.concatenate([a["L3_gnn_fus_b"], a["L3_gnn_attn_b"], a["L3_gnn_fus_b"], a["L3_gnn_fus_b"]]),
        "fus_w": a["L3_gnn_fus_w"].reshape(3, C, C).transpose(1, 0, 2).reshape(C, 3 * C),
        "bn_g": a["L3_gnn_bn_gamma"], "bn_b": a["L3_gnn_bn_beta"],
    }
    arrays["dst"][-1] = N + 1
    for n in range(2):
        for part, name in (("msg", "_msg"), ("edge", "_edge"), ("root", "_root")):
            arrays[f"conv{n}_{part}"] = a[f"L2_gnn_W{n + 1}{name}"]
        arrays[f"conv{n}_b"] = a[f"L2_gnn_b{n + 1}"]
    arrays = {k: np.ascontiguousarray(v) for k, v in arrays.items()}
    t = {k: nc.dram_tensor("in_" + k, v.shape, mybir.dt.from_np(v.dtype), kind="ExternalInput").ap() for k, v in arrays.items()}
    t["out"] = nc.dram_tensor("out", (NP, C), F32, kind="ExternalOutput").ap()
    build(nc, t)
    r = run(nc, [{"in_" + k: v for k, v in arrays.items()}], core_ids=[0])
    return r.results[0]["out"][:N]
```
